# Optimizing a Trainium2 kernel written in Bass

```python
import numpy as np
import jax
import jax.numpy as jnp

def _softmax(x, axis=-1):
    return jax.nn.softmax(x, axis=axis)

def _gelu(x):
    return jax.nn.gelu(x, approximate=True)

def _silu(x):
    return jax.nn.silu(x)

def _sigmoid(x):
    return jax.nn.sigmoid(x)

def _layernorm(x, axis=-1, eps=1e-05):
    m = jnp.mean(x, axis=axis, keepdims=True)
    v = jnp.var(x, axis=axis, keepdims=True)
    return (x - m) / jnp.sqrt(v + eps)

def _scatter_add(tgt, idx, src, axis=0):
    return tgt.at[idx].add(src)

def _segment_sum(src, seg, n):
    return jax.ops.segment_sum(src, seg, n)
kernel_name = 'mk_macaron_d2_jaxref_r8_0972d0'

def setup_inputs(seed: int=0):
    np.random.seed(seed)
    _w = jnp.asarray

    def _L0_attn_setup():
        import jax, jax.numpy as jnp
        import numpy as np
        N_STATE = 64
        SEQ_L = 512
        BATCH, HCH = (16, 64)
        DT_MIN, DT_MAX = (0.001, 0.1)

        def _make_DPLR_HiPPO(N):
            P = np.sqrt(1 + 2 * np.arange(N))
            A = P[:, None] * P[None, :]
            A = np.tril(A) - np.diag(np.arange(N))
            nhippo = -A
            p = 0.5 * np.sqrt(2 * np.arange(1, N + 1) + 1.0)
            q = 2 * p
            S = nhippo + p[:, None] * q[None, :]
            Lambda, V = np.linalg.eig(S)
            Vc = V.conj().T
            p_t = Vc @ p
            q_t = Vc @ q.conj()
            return (Lambda, p_t, q_t, Vc)

        def _ri(z):
            return np.stack([z.real, z.imag], axis=-1).astype(np.float32)

        def _cplx(x_ri):
            return x_ri[..., 0] + 1j * x_ri[..., 1]

        def _s4_kernel(Lambda, p, q, B, Ct, step, L):
            Omega = jnp.exp(-2j * jnp.pi * (jnp.arange(L) / L))
            g = 2.0 / step * ((1.0 - Omega) / (1.0 + Omega))
            c = 2.0 / (1.0 + Omega)
            denom = g[:, None] - Lambda[None, :]
            cauchy = lambda v: (v[None, :] / denom).sum(-1)
            k00 = cauchy(Ct.conj() * B)
            k01 = cauchy(Ct.conj() * p)
            k10 = cauchy(q.conj() * B)
            k11 = cauchy(q.conj() * p)
            at_roots = c * (k00 - k01 * (1.0 / (1.0 + k11)) * k10)
            return jnp.fft.ifft(at_roots, L).real
        key = jax.random.key(seed)
        k_u, k_ct, k_b, k_d, k_ls = jax.random.split(key, 5)
        Lambda, p, q, Vc = _make_DPLR_HiPPO(N_STATE)
        u = jax.random.normal(k_u, (BATCH, HCH, SEQ_L), dtype=jnp.float32)
        Ct_ri = jax.random.normal(k_ct, (1, N_STATE, 2), dtype=jnp.float32) / np.sqrt(N_STATE)
        Bp = jax.random.normal(k_b, (N_STATE, 1), dtype=jnp.float32) / np.sqrt(N_STATE)
        D = jax.random.uniform(k_d, (1,), dtype=jnp.float32)
        log_step = jax.random.uniform(k_ls, (1,), dtype=jnp.float32, minval=np.log(DT_MIN), maxval=np.log(DT_MAX))
        return {'u': u, 'Lambda_ri': jnp.asarray(_ri(Lambda)), 'p_ri': jnp.asarray(_ri(p)), 'q_ri': jnp.asarray(_ri(q)), 'Vc_ri': jnp.asarray(_ri(Vc)), 'Ct_ri': Ct_ri, 'Bp': Bp, 'D': D, 'log_step': log_step}
    _L0_attn_in = _L0_attn_setup()

    def _L0_ffn_setup():
        import jax, jax.numpy as jnp
        import numpy as np
        IN_FEATURES = 512

        def _dequantize(qweight, scale, zero_point):
            N, K_packed = qweight.shape
            groups = K_packed // 3
            p = qweight.reshape(N, groups, 3)
            v0 = p[:, :, 0] & 63
            v1 = p[:, :, 0] >> 6 & 63
            v2 = p[:, :, 1] & 63
            v3 = p[:, :, 2] & 63
            unpacked = jnp.stack([v0, v1, v2, v3], axis=2).reshape(N, groups * 4)
            unpacked = unpacked[:, :IN_FEATURES]
            return (unpacked.astype(jnp.float32) - zero_point) * scale
        key = jax.random.key(seed)
        k1, k2, k3, k4, k5 = jax.random.split(key, 5)
        x = jax.random.normal(k1, (8, 256, 512), dtype=jnp.float32)
        qweight = jax.random.randint(k2, (512, 384), 0, 512, dtype=jnp.int32)
        weight_scale = jax.random.uniform(k3, (512, 1), dtype=jnp.float32) * 0.02 + 0.001
        weight_zero_point = jax.random.uniform(k4, (512, 1), dtype=jnp.float32) * 63.0
        bias = jax.random.normal(k5, (512,), dtype=jnp.float32)
        return {'x': x, 'qweight': qweight, 'weight_scale': weight_scale, 'weight_zero_point': weight_zero_point, 'bias': bias}
    _L0_ffn_in = _L0_ffn_setup()

    def _L1_attn_setup():
        import jax, jax.numpy as jnp
        import numpy as np
        N_STATE = 64
        SEQ_L = 512
        BATCH, HCH = (16, 64)
        DT_MIN, DT_MAX = (0.001, 0.1)

        def _make_DPLR_HiPPO(N):
            P = np.sqrt(1 + 2 * np.arange(N))
            A = P[:, None] * P[None, :]
            A = np.tril(A) - np.diag(np.arange(N))
            nhippo = -A
            p = 0.5 * np.sqrt(2 * np.arange(1, N + 1) + 1.0)
            q = 2 * p
            S = nhippo + p[:, None] * q[None, :]
            Lambda, V = np.linalg.eig(S)
            Vc = V.conj().T
            p_t = Vc @ p
            q_t = Vc @ q.conj()
            return (Lambda, p_t, q_t, Vc)

        def _ri(z):
            return np.stack([z.real, z.imag], axis=-1).astype(np.float32)

        def _cplx(x_ri):
            return x_ri[..., 0] + 1j * x_ri[..., 1]

        def _s4_kernel(Lambda, p, q, B, Ct, step, L):
            Omega = jnp.exp(-2j * jnp.pi * (jnp.arange(L) / L))
            g = 2.0 / step * ((1.0 - Omega) / (1.0 + Omega))
            c = 2.0 / (1.0 + Omega)
            denom = g[:, None] - Lambda[None, :]
            cauchy = lambda v: (v[None, :] / denom).sum(-1)
            k00 = cauchy(Ct.conj() * B)
            k01 = cauchy(Ct.conj() * p)
            k10 = cauchy(q.conj() * B)
            k11 = cauchy(q.conj() * p)
            at_roots = c * (k00 - k01 * (1.0 / (1.0 + k11)) * k10)
            return jnp.fft.ifft(at_roots, L).real
        key = jax.random.key(seed)
        k_u, k_ct, k_b, k_d, k_ls = jax.random.split(key, 5)
        Lambda, p, q, Vc = _make_DPLR_HiPPO(N_STATE)
        u = jax.random.normal(k_u, (BATCH, HCH, SEQ_L), dtype=jnp.float32)
        Ct_ri = jax.random.normal(k_ct, (1, N_STATE, 2), dtype=jnp.float32) / np.sqrt(N_STATE)
        Bp = jax.random.normal(k_b, (N_STATE, 1), dtype=jnp.float32) / np.sqrt(N_STATE)
        D = jax.random.uniform(k_d, (1,), dtype=jnp.float32)
        log_step = jax.random.uniform(k_ls, (1,), dtype=jnp.float32, minval=np.log(DT_MIN), maxval=np.log(DT_MAX))
        return {'u': u, 'Lambda_ri': jnp.asarray(_ri(Lambda)), 'p_ri': jnp.asarray(_ri(p)), 'q_ri': jnp.asarray(_ri(q)), 'Vc_ri': jnp.asarray(_ri(Vc)), 'Ct_ri': Ct_ri, 'Bp': Bp, 'D': D, 'log_step': log_step}
    _L1_attn_in = _L1_attn_setup()

    def _L1_ffn_setup():
        import jax, jax.numpy as jnp
        import numpy as np
        D = 512
        F = 1376
        B, S = (4, 256)
        key = jax.random.key(seed)
        k_x, k_g, k_u, k_d = jax.random.split(key, 4)
        scale = 0.02
        return {'x': jax.random.normal(k_x, (B, S, D), dtype=jnp.float32), 'W_gate': jax.random.normal(k_g, (F, D), dtype=jnp.float32) * scale, 'W_up': jax.random.normal(k_u, (F, D), dtype=jnp.float32) * scale, 'W_down': jax.random.normal(k_d, (D, F), dtype=jnp.float32) * scale}
    _L1_ffn_in = _L1_ffn_setup()
    _d = {'L0_attn_u': _L0_attn_in['u'], 'L0_attn_Lambda_ri': _L0_attn_in['Lambda_ri'], 'L0_attn_p_ri': _L0_attn_in['p_ri'], 'L0_attn_q_ri': _L0_attn_in['q_ri'], 'L0_attn_Vc_ri': _L0_attn_in['Vc_ri'], 'L0_attn_Ct_ri': _L0_attn_in['Ct_ri'], 'L0_attn_Bp': _L0_attn_in['Bp'], 'L0_attn_D': _L0_attn_in['D'], 'L0_attn_log_step': _L0_attn_in['log_step'], 'L0_ffn_qweight': _L0_ffn_in['qweight'], 'L0_ffn_weight_scale': _L0_ffn_in['weight_scale'], 'L0_ffn_weight_zero_point': _L0_ffn_in['weight_zero_point'], 'L0_ffn_bias': _L0_ffn_in['bias'], 'L1_attn_Lambda_ri': _L1_attn_in['Lambda_ri'], 'L1_attn_p_ri': _L1_attn_in['p_ri'], 'L1_attn_q_ri': _L1_attn_in['q_ri'], 'L1_attn_Vc_ri': _L1_attn_in['Vc_ri'], 'L1_attn_Ct_ri': _L1_attn_in['Ct_ri'], 'L1_attn_Bp': _L1_attn_in['Bp'], 'L1_attn_D': _L1_attn_in['D'], 'L1_attn_log_step': _L1_attn_in['log_step'], 'L1_ffn_W_gate': _L1_ffn_in['W_gate'], 'L1_ffn_W_up': _L1_ffn_in['W_up'], 'L1_ffn_W_down': _L1_ffn_in['W_down']}
    _x0 = _d['L0_attn_u']
    _d['L0_attn_u'] = jax.random.normal(jax.random.fold_in(jax.random.key(seed), 1), (1, 2048, 512), dtype=_x0.dtype)
    del _x0
    return _d

def reference(L0_attn_u, L0_attn_Lambda_ri, L0_attn_p_ri, L0_attn_q_ri, L0_attn_Vc_ri, L0_attn_Ct_ri, L0_attn_Bp, L0_attn_D, L0_attn_log_step, L0_ffn_qweight, L0_ffn_weight_scale, L0_ffn_weight_zero_point, L0_ffn_bias, L1_attn_Lambda_ri, L1_attn_p_ri, L1_attn_q_ri, L1_attn_Vc_ri, L1_attn_Ct_ri, L1_attn_Bp, L1_attn_D, L1_attn_log_step, L1_ffn_W_gate, L1_ffn_W_up, L1_ffn_W_down):

    def _L0_attn_ref(u, Lambda_ri, p_ri, q_ri, Vc_ri, Ct_ri, Bp, D, log_step):
        import jax, jax.numpy as jnp
        import numpy as np
        N_STATE = 64
        SEQ_L = 512
        BATCH, HCH = (16, 64)
        DT_MIN, DT_MAX = (0.001, 0.1)

        def _make_DPLR_HiPPO(N):
            P = np.sqrt(1 + 2 * np.arange(N))
            A = P[:, None] * P[None, :]
            A = np.tril(A) - np.diag(np.arange(N))
            nhippo = -A
            p = 0.5 * np.sqrt(2 * np.arange(1, N + 1) + 1.0)
            q = 2 * p
            S = nhippo + p[:, None] * q[None, :]
            Lambda, V = np.linalg.eig(S)
            Vc = V.conj().T
            p_t = Vc @ p
            q_t = Vc @ q.conj()
            return (Lambda, p_t, q_t, Vc)

        def _ri(z):
            return np.stack([z.real, z.imag], axis=-1).astype(np.float32)

        def _cplx(x_ri):
            return x_ri[..., 0] + 1j * x_ri[..., 1]

        def _s4_kernel(Lambda, p, q, B, Ct, step, L):
            Omega = jnp.exp(-2j * jnp.pi * (jnp.arange(L) / L))
            g = 2.0 / step * ((1.0 - Omega) / (1.0 + Omega))
            c = 2.0 / (1.0 + Omega)
            denom = g[:, None] - Lambda[None, :]
            cauchy = lambda v: (v[None, :] / denom).sum(-1)
            k00 = cauchy(Ct.conj() * B)
            k01 = cauchy(Ct.conj() * p)
            k10 = cauchy(q.conj() * B)
            k11 = cauchy(q.conj() * p)
            at_roots = c * (k00 - k01 * (1.0 / (1.0 + k11)) * k10)
            return jnp.fft.ifft(at_roots, L).real
        L = u.shape[-1]
        Lambda = _cplx(Lambda_ri)
        p = _cplx(p_ri)
        q = _cplx(q_ri)
        Vc = _cplx(Vc_ri)
        Ct = _cplx(Ct_ri).reshape(-1)
        B = (Vc @ Bp.astype(Vc.dtype)).reshape(-1)
        step = jnp.exp(log_step)[0]
        K = _s4_kernel(Lambda, p, q, B, Ct, step, L).astype(u.dtype)
        n = 2 * L
        y = jnp.fft.irfft(jnp.fft.rfft(u, n=n) * jnp.fft.rfft(K, n=n), n=n)[..., :L]
        return y + D[0] * u

    def _L0_ffn_ref(x, qweight, weight_scale, weight_zero_point, bias):
        import jax, jax.numpy as jnp
        import numpy as np
        IN_FEATURES = 512

        def _dequantize(qweight, scale, zero_point):
            N, K_packed = qweight.shape
            groups = K_packed // 3
            p = qweight.reshape(N, groups, 3)
            v0 = p[:, :, 0] & 63
            v1 = p[:, :, 0] >> 6 & 63
            v2 = p[:, :, 1] & 63
            v3 = p[:, :, 2] & 63
            unpacked = jnp.stack([v0, v1, v2, v3], axis=2).reshape(N, groups * 4)
            unpacked = unpacked[:, :IN_FEATURES]
            return (unpacked.astype(jnp.float32) - zero_point) * scale
        w = _dequantize(qweight, weight_scale, weight_zero_point)
        return jnp.einsum('bsk,nk->bsn', x, w) + bias

    def _L1_attn_ref(u, Lambda_ri, p_ri, q_ri, Vc_ri, Ct_ri, Bp, D, log_step):
        import jax, jax.numpy as jnp
        import numpy as np
        N_STATE = 64
        SEQ_L = 512
        BATCH, HCH = (16, 64)
        DT_MIN, DT_MAX = (0.001, 0.1)

        def _make_DPLR_HiPPO(N):
            P = np.sqrt(1 + 2 * np.arange(N))
            A = P[:, None] * P[None, :]
            A = np.tril(A) - np.diag(np.arange(N))
            nhippo = -A
            p = 0.5 * np.sqrt(2 * np.arange(1, N + 1) + 1.0)
            q = 2 * p
            S = nhippo + p[:, None] * q[None, :]
            Lambda, V = np.linalg.eig(S)
            Vc = V.conj().T
            p_t = Vc @ p
            q_t = Vc @ q.conj()
            return (Lambda, p_t, q_t, Vc)

        def _ri(z):
            return np.stack([z.real, z.imag], axis=-1).astype(np.float32)

        def _cplx(x_ri):
            return x_ri[..., 0] + 1j * x_ri[..., 1]

        def _s4_kernel(Lambda, p, q, B, Ct, step, L):
            Omega = jnp.exp(-2j * jnp.pi * (jnp.arange(L) / L))
            g = 2.0 / step * ((1.0 - Omega) / (1.0 + Omega))
            c = 2.0 / (1.0 + Omega)
            denom = g[:, None] - Lambda[None, :]
            cauchy = lambda v: (v[None, :] / denom).sum(-1)
            k00 = cauchy(Ct.conj() * B)
            k01 = cauchy(Ct.conj() * p)
            k10 = cauchy(q.conj() * B)
            k11 = cauchy(q.conj() * p)
            at_roots = c * (k00 - k01 * (1.0 / (1.0 + k11)) * k10)
            return jnp.fft.ifft(at_roots, L).real
        L = u.shape[-1]
        Lambda = _cplx(Lambda_ri)
        p = _cplx(p_ri)
        q = _cplx(q_ri)
        Vc = _cplx(Vc_ri)
        Ct = _cplx(Ct_ri).reshape(-1)
        B = (Vc @ Bp.astype(Vc.dtype)).reshape(-1)
        step = jnp.exp(log_step)[0]
        K = _s4_kernel(Lambda, p, q, B, Ct, step, L).astype(u.dtype)
        n = 2 * L
        y = jnp.fft.irfft(jnp.fft.rfft(u, n=n) * jnp.fft.rfft(K, n=n), n=n)[..., :L]
        return y + D[0] * u

    def _L1_ffn_ref(x, W_gate, W_up, W_down):
        import jax, jax.numpy as jnp
        import numpy as np
        D = 512
        F = 1376
        B, S = (4, 256)
        out_shape = x.shape[:-1] + (W_down.shape[0],)
        xt = x.reshape(-1, x.shape[-1])
        up = xt @ W_up.T
        gate = jax.nn.silu(xt @ W_gate.T)
        y = gate * up @ W_down.T
        return y.reshape(out_shape)
    x = L0_attn_u
    x = x + 0.5 * _L0_ffn_ref(_layernorm(x, axis=-1), L0_ffn_qweight, L0_ffn_weight_scale, L0_ffn_weight_zero_point, L0_ffn_bias)
    x = x + _L0_attn_ref(_layernorm(x, axis=-1), L0_attn_Lambda_ri, L0_attn_p_ri, L0_attn_q_ri, L0_attn_Vc_ri, L0_attn_Ct_ri, L0_attn_Bp, L0_attn_D, L0_attn_log_step)
    x = x + 0.5 * _L0_ffn_ref(_layernorm(x, axis=-1), L0_ffn_qweight, L0_ffn_weight_scale, L0_ffn_weight_zero_point, L0_ffn_bias)
    x = x + 0.5 * _L1_ffn_ref(_layernorm(x, axis=-1), L1_ffn_W_gate, L1_ffn_W_up, L1_ffn_W_down)
    x = x + _L1_attn_ref(_layernorm(x, axis=-1), L1_attn_Lambda_ri, L1_attn_p_ri, L1_attn_q_ri, L1_attn_Vc_ri, L1_attn_Ct_ri, L1_attn_Bp, L1_attn_D, L1_attn_log_step)
    x = x + 0.5 * _L1_ffn_ref(_layernorm(x, axis=-1), L1_ffn_W_gate, L1_ffn_W_up, L1_ffn_W_down)
    return x

_drawn_inputs = setup_inputs


def setup_inputs(seed=0):
    import zlib

    import numpy as np

    out = dict(_drawn_inputs(seed))
    spreads = {}
    factors = {'L0_attn_Lambda_ri': 8.0,
     'L0_attn_p_ri': 8.0,
     'L0_attn_q_ri': 8.0,
     'L0_attn_Vc_ri': 8.0,
     'L0_attn_Ct_ri': 8.0,
     'L0_attn_Bp': 8.0,
     'L0_ffn_weight_zero_point': 8.0,
     'L1_attn_Lambda_ri': 8.0,
     'L1_attn_p_ri': 8.0,
     'L1_attn_q_ri': 8.0,
     'L1_attn_Vc_ri': 8.0,
     'L1_attn_Ct_ri': 8.0,
     'L1_attn_Bp': 8.0,
     'L1_ffn_W_gate': 3.593,
     'L1_ffn_W_up': 3.488,
     'L1_ffn_W_down': 3.462}
    for name, (base, spread) in spreads.items():
        noise = np.random.default_rng([zlib.crc32(name.encode()), seed]).standard_normal(out[name].shape)
        drawn = base * np.exp(spread * noise) if base else spread * noise
        out[name] = jnp.asarray(drawn.astype(out[name].dtype))
    for name, factor in factors.items():
        out[name] = (out[name] * factor).astype(out[name].dtype)
    return out
```

```python
from contextlib import ExitStack

import numpy as np
import concourse.bass as bass
from concourse import mybir

F32 = mybir.dt.float32
F32R = mybir.dt.float32r
I32 = mybir.dt.int32
ALU = mybir.AluOpType
ACT = mybir.ActivationFunctionType
AX = mybir.AxisListType

P = 128
ROWS = 2048
D = 512
F = 1376
NS = 64
EPS = 1e-5
TILES = ROWS // P
KT = D // P
FT = (F + P - 1) // P
BLK = 4
STATS_AHEAD, NORM_AHEAD, XT_AHEAD = 6, 5, 4
SLOTS = 4

GATE0, UP0, DOWN0 = 0, KT * F, 2 * KT * F
WCOLS = DOWN0 + FT * D
CHUNK = 520
NCHUNK = WCOLS // CHUNK
EARLY_CHUNKS = 28
assert NCHUNK * CHUNK == WCOLS

(LAM_R, LAM_I, P_R, P_I, Q_R, Q_I, CT_R, CT_I, LOGSTEP, D_0, D_1) = range(11)
VC0 = 12
BP0 = VC0 + 2 * NS
PARCOLS = BP0 + NS


def fwidth(f):
    return min(P, F - f * P)


def build(nc, x_in, params, qweight, qshift, qscale, qzero, qbias, wffn,
          cos_in, sin_in, omega_in, one_plus_in, diag_in, out):
    with ExitStack() as ctx:
        cursor = [(nc.sbuf_base + 31) // 32 * 32]
        counter = [0]

        def sb(name, shape, dt):
            size = int(np.prod(shape[1:])) * 4
            t = nc.alloc_sbuf_tensor_at(name, shape, dt, offset=cursor[0])
            at = cursor[0]
            cursor[0] += (size + 31) // 32 * 32
            return t, at

        def overlay(name, shape, dt, at):
            return nc.alloc_sbuf_tensor_at(name, shape, dt, offset=at)

        def sem(name):
            return ctx.enter_context(nc.semaphore(name))

        Wh, wh_at = sb("ffn_w_hi", [P, WCOLS], F32R)
        Wl, wl_at = sb("ffn_w_lo", [P, WCOLS], F32R)
        X, _ = sb("x_rows", [P, TILES, D], F32)
        TOEh, _ = sb("toeplitz_hi", [P, 2, D], F32R)
        TOEl, _ = sb("toeplitz_lo", [P, 2, D], F32R)
        XTh, _ = sb("xt_hi", [P, KT, SLOTS, P], F32R)
        XTl, _ = sb("xt_lo", [P, KT, SLOTS, P], F32R)
        LN, _ = sb("normalised", [P, SLOTS, D], F32)
        Hh, h_at = sb("hidden_hi", [P, 2, D], F32R)
        Hl, _ = sb("hidden_lo", [P, 2, D], F32R)
        G, _ = sb("gated", [P, 2, CHUNK], F32)
        ident, _ = sb("identity", [P, P], F32)
        bnst, _ = sb("bn_stats", [P, SLOTS, 6], F32)
        mv, _ = sb("mean_var", [P, SLOTS, 2], F32)
        veps, _ = sb("var_eps", [P, SLOTS, 1], F32)
        rstd, _ = sb("rstd", [P, SLOTS, 1], F32)
        nmr, _ = sb("minus_mean_rstd", [P, SLOTS, 1], F32)
        mr, _ = sb("mean_rstd", [P, SLOTS, 1], F32)
        consts, _ = sb("eps_minushalf_minusone", [P, 3], F32)
        assert cursor[0] <= nc.sbuf_usable_end, (cursor[0], nc.sbuf_usable_end)

        tail = EARLY_CHUNKS * CHUNK * 4
        Qh = overlay("dequant_hi", [P, KT, D], F32R, h_at)
        Ql = overlay("dequant_lo", [P, KT, D], F32R, wl_at + tail)
        biasB = overlay("half_bias", [P, D], F32, wh_at + tail)

        sc = [wh_at]

        def scratch(name, shape, dt=F32):
            t = overlay(name, shape, dt, sc[0])
            sc[0] += (int(np.prod(shape[1:])) * 4 + 31) // 32 * 32
            return t

        par = scratch("s4_params", [P, PARCOLS])
        cosT = scratch("cos_table", [P, KT, D])
        sinT = scratch("sin_table", [P, KT, D])
        om = scratch("omega_terms", [P, 3, D])
        npl = scratch("one_plus_omega", [P, 2, KT])
        diag = scratch("causal_and_diagonal", [P, 2, P])
        qraw = scratch("q_raw", [P, KT, D], I32)
        qsh = scratch("q_shift", [P, 1], I32)
        wq = scratch("dequant_f32", [P, KT, D])
        zpB = scratch("zero_point_rows", [P, D])
        assert sc[0] <= wh_at + tail
        sc[0] = wl_at
        scB = scratch("scale_rows", [P, D])
        den_r = scratch("den_r", [P, D])
        den_i = scratch("den_i", [P, D])
        mag = scratch("den_abs2", [P, D])
        tmp = scratch("den_tmp", [P, D])
        Rr = scratch("inv_den_r", [P, D])
        Ri = scratch("inv_den_i", [P, D])
        bprod = scratch("b_products", [P, 2, NS])
        vec = scratch("b_and_p", [P, 2, 2])
        small = scratch("s4_small", [P, 16])
        num_r = scratch("numer_r", [P, 2, 2])
        num_i = scratch("numer_i", [P, 2, 2])
        rhs1 = scratch("cauchy_rhs_re", [P, 2, 8])
        rhs2 = scratch("cauchy_rhs_im", [P, 2, 8])
        kk = scratch("cauchy_sums", [P, KT, 2, 8])
        cm = scratch("complex_work", [P, 16, KT, 2])
        at_r = scratch("at_roots_r", [P, KT, 2])
        at_i = scratch("at_roots_i", [P, KT, 2])
        tw = scratch("twist_tmp", [P, P])
        A1 = scratch("twisted_1", [P, 2, KT, P])
        A2 = scratch("twisted_2", [P, 2, KT, P])
        toe = scratch("toeplitz_f32", [P, 2, D])
        assert sc[0] <= wl_at + tail

        front = [ctx.enter_context(nc.psum_tensor(f"front{i}", [P, D], F32)) for i in range(4)]
        acc = [ctx.enter_context(nc.psum_tensor(f"acc{i}", [P, D], F32)) for i in range(BLK)]

        params_in = sem("params_in")
        quant_in = sem("quant_in")
        tables_in = sem("tables_in")
        x_loaded = sem("x_loaded")
        chunk_in = [sem("chunk_in_even"), sem("chunk_in_odd")]
        chunk_hi = sem("chunk_hi")
        chunk_split = sem("chunk_split")
        setup_dve = sem("setup_dve")
        step_exp = sem("step_exp")
        inv_den_ready = sem("inv_den_ready")
        cauchy_ready = sem("cauchy_ready")
        toeplitz_sum = sem("toeplitz_sum")
        dequant_ready = sem("dequant_ready")
        dequant_hi = sem("dequant_hi")
        toe_hi = sem("toe_hi")
        toe_ready = sem("toe_ready")
        quant_split = sem("quant_split")
        const_ready = sem("const_ready")
        stats_raw = sem("stats_raw")
        stats_ready = sem("stats_ready")
        eps_added = sem("eps_added")
        rstd_made = sem("rstd_made")
        mr_made = sem("mr_made")
        rstd_ready = sem("rstd_ready")
        norm_done = sem("norm_done")
        transposed = sem("transposed")
        xt_hi_done = sem("xt_hi_done")
        xt_ready = sem("xt_ready")
        bias_added = sem("bias_added")
        acc_ready = sem("acc_ready")
        x_updated = sem("x_updated")
        gate_ready = sem("gate_ready")
        up_ready = sem("up_ready")
        silu_done = sem("silu_done")
        prod_done = sem("prod_done")
        hid_hi_done = sem("hid_hi_done")
        hid_ready = sem("hid_ready")
        down_done = sem("down_done")
        stored = sem("stored")

        block = ctx.enter_context(nc.Block())

        x_v = x_in.rearrange("o (t p) d -> p (o t) d", p=P)
        out_v = out.rearrange("o (t p) d -> p (o t) d", p=P)

        LIGHT = {0: ("quant", 0), 1: ("conv", 0), 2: ("quant", 0), 4: ("conv", 1)}
        CHUNKS_IN = {1: (0, TILES), 2: (TILES, EARLY_CHUNKS - TILES)}
        X_UP0 = 2
        BLOCKS_BEFORE = {3: 0, 5: TILES // BLK}
        BIAS_BEFORE = {0: 0, 2: TILES}


        def x_tile(t, ahead=0):
            if isinstance(t, int):
                at = (t + ahead) % TILES
                return X[:, at:at + 1, :].rearrange("p o d -> p (o d)")
            return X[:, bass.ds((t + ahead) % TILES if ahead else t, 1), :].rearrange("p o d -> p (o d)")

        def stats_step(dve, v0, t, s, ahead=0):
            slot = (s + ahead) % SLOTS
            v = v0 + t + ahead
            if v0:
                dve.wait_ge(x_updated, X_UP0 + v - TILES + 1)
            elif not isinstance(t, int):
                dve.wait_ge(x_updated, t - s + 1)
            if v0 or not isinstance(t, int) or v >= SLOTS:
                dve.wait_ge(norm_done, v - SLOTS + 1)
            nc.vector.bn_stats(bnst[:, slot, :], x_tile(t, ahead)).then_inc(stats_raw, 1)

        def stats_halves_written(dve, v0, t, ahead=0):
            dve.wait_ge(stats_raw, v0 + t + ahead + 1)

        def aggregate_step(s, ahead=0):
            slot = (s + ahead) % SLOTS
            nc.vector.bn_aggr(mv[:, slot, :], bnst[:, slot, :]).then_inc(stats_ready, 1)

        def rstd_step(pool, v0, t, s, ahead=0):
            slot = (s + ahead) % SLOTS
            v = v0 + t + ahead
            pool.wait_ge(stats_ready, v + 1)
            nc.gpsimd.tensor_tensor(veps[:, slot, :], mv[:, slot, 1:2], consts[:, 0:1], ALU.add).then_inc(eps_added, 1)
            pool.wait_ge(eps_added, v + 1)
            nc.gpsimd.tensor_tensor(rstd[:, slot, :], veps[:, slot, :], consts[:, 1:2], ALU.pow).then_inc(rstd_made, 1)
            pool.wait_ge(rstd_made, v + 1)
            nc.gpsimd.tensor_tensor(mr[:, slot, :], mv[:, slot, 0:1], rstd[:, slot, :], ALU.mult).then_inc(mr_made, 1)
            pool.wait_ge(mr_made, v + 1)
            nc.gpsimd.tensor_tensor(nmr[:, slot, :], mr[:, slot, :], consts[:, 2:3], ALU.mult).then_inc(rstd_ready, 1)

        def norm_step(act, v0, t, s, ahead=0):
            slot = (s + ahead) % SLOTS
            v = v0 + t + ahead
            if v0 or not isinstance(t, int) or v >= SLOTS:
                act.wait_ge(transposed, v - SLOTS + 1)
            act.wait_ge(rstd_ready, v + 1)
            nc.scalar.activation(LN[:, slot, :], x_tile(t, ahead), ACT.Identity, bias=nmr[:, slot, :],
                                 scale=rstd[:, slot, :]).then_inc(norm_done, 1)

        def transpose_step(pe, v0, t, s, ahead=0):
            slot = (s + ahead) % SLOTS
            pe.wait_ge(norm_done, v0 + t + ahead + 1)
            for j in range(KT):
                last = nc.tensor.transpose(front[slot][:, j * P:(j + 1) * P],
                                           LN[:, slot, j * P:(j + 1) * P], ident[:])
            last.then_inc(transposed, 1)

        def bank(slot):
            return front[slot][:, :].rearrange("p (j r) -> p j r", j=KT)

        def xt_hi_step(act, v0, t, s, ahead=0):
            slot = (s + ahead) % SLOTS
            act.wait_ge(transposed, v0 + t + ahead + 1)
            nc.scalar.activation(XTh[:, :, slot, :], bank(slot), ACT.Copy).then_inc(xt_hi_done, 1)

        def xt_lo_step(dve, v0, t, s, ahead=0):
            slot = (s + ahead) % SLOTS
            dve.wait_ge(xt_hi_done, v0 + t + ahead + 1)
            nc.vector.tensor_tensor(XTl[:, :, slot, :], bank(slot), XTh[:, :, slot, :].bitcast(F32),
                                    ALU.subtract).then_inc(xt_ready, 1)

        def update_step(dve, v0, t, a, scale):
            dve.wait_ge(acc_ready, v0 + t + 1)
            xt = x_tile(t)
            if scale == 1.0:
                nc.vector.tensor_tensor(xt, acc[a][:], xt, ALU.add).then_inc(x_updated, 1)
            else:
                nc.vector.scalar_tensor_tensor(out=xt, in0=acc[a][:], scalar=scale, in1=xt,
                                               op0=ALU.mult, op1=ALU.add).then_inc(x_updated, 1)

        @block.sync
        def _(sp):
            sp.dma_start(par[:], params).then_inc(params_in, 16)
            sp.dma_start(om[:], omega_in.partition_broadcast(P)).then_inc(params_in, 16)
            sp.dma_start(qraw[:], qweight).then_inc(quant_in, 16)
            sp.dma_start(qsh[:], qshift).then_inc(quant_in, 16)
            sp.dma_start(zpB[:], qzero.partition_broadcast(P)).then_inc(quant_in, 16)
            sp.dma_start(scB[:], qscale.partition_broadcast(P)).then_inc(quant_in, 16)
            sp.dma_start(biasB[:], qbias.partition_broadcast(P)).then_inc(quant_in, 16)
            sp.dma_start(ident[:], diag_in[:, 1, :]).then_inc(tables_in, 16)
            sp.dma_start(npl[:], one_plus_in).then_inc(tables_in, 16)
            sp.dma_start(diag[:], diag_in).then_inc(tables_in, 16)
            sp.dma_start(cosT[:], cos_in).then_inc(tables_in, 16)
            sp.dma_start(sinT[:], sin_in).then_inc(tables_in, 16)
            for g in range(TILES // BLK):
                sp.dma_start(X[:, g * BLK:(g + 1) * BLK, :], x_v[:, g * BLK:(g + 1) * BLK, :]).then_inc(x_loaded, 16)
            sp.wait_ge(toe_ready, 2)
            sp.wait_ge(quant_split, 1)
            sp.dma_start(G[:, 0, :], wffn[:, 0:CHUNK]).then_inc(chunk_in[0], 16)
            sp.dma_start(G[:, 1, :], wffn[:, CHUNK:2 * CHUNK]).then_inc(chunk_in[1], 16)
            with sp.Fori(1, NCHUNK // 2) as pair:
                for parity in range(2):
                    sp.wait_ge(chunk_split, pair * 2 + parity - 1)
                    sp.dma_start(G[:, parity, :], wffn[:, bass.ds((pair * 2 + parity) * CHUNK, CHUNK)]
                                 ).then_inc(chunk_in[parity], 16)
            for b in range(TILES // BLK):
                sp.wait_ge(x_updated, X_UP0 + 5 * TILES + (b + 1) * BLK)
                sp.dma_start(out_v[:, b * BLK:(b + 1) * BLK, :], X[:, b * BLK:(b + 1) * BLK, :]).then_inc(stored, 16)
            sp.wait_ge(stored, 16 * (TILES // BLK))

        def chunk_lo_step(pool, c, half):
            parity = half
            pool.wait_ge(chunk_hi, c + 1)
            cols = bass.ds(c * CHUNK, CHUNK)
            nc.gpsimd.tensor_tensor(Wl[:, cols], G[:, parity, :], Wh[:, cols].bitcast(F32),
                                    ALU.subtract).then_inc(chunk_split, 1)

        @block.gpsimd
        def _(pool):
            for i, value in enumerate((EPS, -0.5, -1.0)):
                nc.gpsimd.memset(consts[:, i:i + 1], value).then_inc(const_ready, 1)
            pool.wait_ge(const_ready, 3)
            for t in range(STATS_AHEAD):
                rstd_step(pool, 0, t, t % SLOTS)

            def light(stage, first, last, chunks):
                kind, _ = LIGHT[stage]
                v0 = stage * TILES
                with pool.Fori(first // SLOTS, last // SLOTS) as grp:
                    t = grp * SLOTS
                    for s in range(SLOTS):
                        rstd_step(pool, v0, t + s, s, STATS_AHEAD)
                        if kind == "quant":
                            xt = x_tile(t + s)
                            pool.wait_ge(norm_done, v0 + t + s + 1)
                            nc.gpsimd.tensor_tensor(xt, xt, biasB[:], ALU.add).then_inc(bias_added, 1)
                        if chunks:
                            chunk_lo_step(pool, CHUNKS_IN[stage][0] + t + s, s % 2)

            pool.wait_ge(quant_split, 1)
            light(0, 0, TILES, False)
            light(1, 0, TILES, True)
            light(2, 0, CHUNKS_IN[2][1], True)
            light(2, CHUNKS_IN[2][1], TILES, False)
            pool.wait_ge(acc_ready, 3 * TILES)
            for c in range(EARLY_CHUNKS, NCHUNK):
                chunk_lo_step(pool, c, c % 2)

            def ffn(stage, first, last, ends=False):
                v0 = stage * TILES
                with pool.Fori(first // SLOTS, last // SLOTS) as grp:
                    t = grp * SLOTS
                    for s in range(BLK):
                        rstd_step(pool, v0, t + s, s, STATS_AHEAD)

            ffn(3, 0, TILES)
            light(4, 0, TILES, False)
            ffn(5, 0, TILES - BLK)

        @block.scalar
        def _(act):
            def chunk_hi_step(c, parity):
                act.wait_ge(chunk_in[parity], 16 * (c // 2 + 1) if isinstance(c, int) else c * 8 + 16 - 8 * parity)
                cols = bass.ds(c * CHUNK, CHUNK)
                nc.scalar.activation(Wh[:, cols], G[:, parity, :], ACT.Copy).then_inc(chunk_hi, 1)

            act.wait_ge(params_in, 32)
            nc.scalar.activation(small[:, 0:1], par[:, LOGSTEP:LOGSTEP + 1], ACT.Exp, scale=-1.0).then_inc(step_exp, 1)
            act.wait_ge(dequant_ready, 1)
            nc.scalar.activation(Qh[:], wq[:], ACT.Copy).then_inc(dequant_hi, 1)
            for layer in range(2):
                act.wait_ge(toe_hi, layer + 1)
                nc.scalar.activation(TOEh[:, layer, :], toe[:, layer, :], ACT.Copy).then_inc(toe_ready, 1)
            for t in range(NORM_AHEAD):
                if t == SLOTS:
                    for u in range(XT_AHEAD):
                        xt_hi_step(act, 0, u, u)
                norm_step(act, 0, t, t % SLOTS)

            def light(stage, first, last, chunks):
                v0 = stage * TILES
                with act.Fori(first // SLOTS, last // SLOTS) as grp:
                    t = grp * SLOTS
                    for s in range(SLOTS):
                        norm_step(act, v0, t + s, s, NORM_AHEAD)
                        act.wait_ge(acc_ready, v0 + t + s + 1)
                        xt_hi_step(act, v0, t + s, s, XT_AHEAD)
                        if chunks:
                            chunk_hi_step(CHUNKS_IN[stage][0] + t + s, s % 2)

            light(0, 0, TILES, False)
            light(1, 0, TILES, True)
            light(2, 0, CHUNKS_IN[2][1], True)
            light(2, CHUNKS_IN[2][1], TILES, False)
            act.wait_ge(acc_ready, 3 * TILES)
            act.wait_ge(bias_added, 2 * TILES)
            for c in range(EARLY_CHUNKS, NCHUNK):
                chunk_hi_step(c, c % 2)

            def ffn(stage, first, last, ahead=True):
                v0 = stage * TILES
                k0 = BLOCKS_BEFORE[stage]
                with act.Fori(first // SLOTS, last // SLOTS) as grp:
                    t = grp * SLOTS
                    for f in range(FT):
                        m = fwidth(f)
                        n = (k0 * FT + f) + grp * FT
                        act.wait_ge(gate_ready, n + 1)
                        if stage == 3:
                            if f < 2:
                                act.wait_ge(chunk_split, NCHUNK)
                        if stage != 3 or f >= 2:
                            act.wait_ge(hid_ready, n - 1)
                        nc.scalar.activation(G[:m, f % 2, 0:D], front[2 * (f % 2)][:m, :], ACT.Silu
                                             ).then_inc(silu_done, 1)
                        act.wait_ge(prod_done, n + 1)
                        if f == 1:
                            act.wait_ge(acc_ready, v0 + t)
                        elif f >= 2:
                            act.wait_ge(down_done, (FT - 1) * (k0 + grp) + f - 1)
                        elif stage == 5:
                            act.wait_ge(down_done, (FT - 1) * (k0 + grp))
                        nc.scalar.activation(Hh[:m, f % 2, :], G[:m, f % 2, 0:D], ACT.Copy).then_inc(hid_hi_done, 1)
                        if 3 <= f < 6 and ahead:
                            norm_step(act, v0, t + f - 3, f - 3, NORM_AHEAD)
                    for s in range(BLK):
                        if ahead:
                            xt_hi_step(act, v0, t + s, s, XT_AHEAD)
                    if ahead:
                        norm_step(act, v0, t + 3, 3, NORM_AHEAD)

            ffn(3, 0, TILES)
            light(4, 0, TILES, False)
            ffn(5, 0, TILES - BLK)
            ffn(5, TILES - BLK, TILES, ahead=False)

        @block.vector
        def _(dve):
            chain = [0]

            def link(ins):
                chain[0] += 1
                ins.then_inc(setup_dve, 1)
                dve.wait_ge(setup_dve, chain[0])

            V = nc.vector

            dve.wait_ge(quant_in, 80)
            link(V.tensor_scalar(qraw[:], qraw[:], qsh[:, 0:1], 63, ALU.logical_shift_right, ALU.bitwise_and))
            link(V.tensor_tensor(wq[:], qraw[:], zpB[:].unsqueeze(1).to_broadcast([P, KT, D]), ALU.subtract))
            link(V.tensor_scalar(scB[:], scB[:], 0.5, None, ALU.mult))
            link(V.tensor_scalar(biasB[:], biasB[:], 0.5, None, ALU.mult))
            V.tensor_tensor(wq[:], wq[:], scB[:].unsqueeze(1).to_broadcast([P, KT, D]), ALU.mult
                            ).then_inc(dequant_ready, 1)
            dve.wait_ge(dequant_hi, 1)
            V.tensor_tensor(Ql[:], wq[:], Qh[:].bitcast(F32), ALU.subtract).then_inc(quant_split, 1)

            def col(c):
                return par[:, c:c + 1]

            dve.wait_ge(params_in, 32)
            vc = par[:, VC0:VC0 + 2 * NS].rearrange("p (c m) -> p c m", c=2)
            bp = par[:, BP0:BP0 + NS].unsqueeze(1).to_broadcast([P, 2, NS])
            link(V.tensor_tensor(bprod[:], vc, bp, ALU.mult))
            link(V.tensor_reduce(vec[:, :, 0:1], bprod[:], AX.X, ALU.add))
            link(V.tensor_copy(vec[:, 0, 1:2], col(P_R)))
            link(V.tensor_copy(vec[:, 1, 1:2], col(P_I)))
            for a, (ur, ui) in enumerate(((CT_R, CT_I), (Q_R, Q_I))):
                link(V.tensor_scalar(small[:, 4:6], vec[:, 0, :], col(ur), None, ALU.mult))
                link(V.scalar_tensor_tensor(out=num_r[:, a, :], in0=vec[:, 1, :], scalar=col(ui), in1=small[:, 4:6],
                                            op0=ALU.mult, op1=ALU.add))
                link(V.tensor_scalar(small[:, 6:8], vec[:, 0, :], col(ui), None, ALU.mult))
                link(V.scalar_tensor_tensor(out=num_i[:, a, :], in0=vec[:, 1, :], scalar=col(ur), in1=small[:, 6:8],
                                            op0=ALU.mult, op1=ALU.subtract))
            link(V.memset(rhs1[:], 0.0))
            link(V.memset(rhs2[:], 0.0))
            for layer in range(2):
                p0 = layer * NS
                rows = slice(p0, p0 + NS)
                nr = num_r[rows, :, :].rearrange("p a b -> p (a b)")
                ni = num_i[rows, :, :].rearrange("p a b -> p (a b)")
                link(V.tensor_copy(rhs1[rows, layer, 0:4], nr))
                link(V.tensor_copy(rhs1[rows, layer, 4:8], ni))
                link(V.tensor_scalar(rhs2[rows, layer, 0:4], ni, -1.0, None, ALU.mult))
                link(V.tensor_copy(rhs2[rows, layer, 4:8], nr))

            dve.wait_ge(step_exp, 1)
            a2, nlr, nli, nal = (small[:, i:i + 1] for i in (1, 2, 3, 8))
            link(V.tensor_scalar(a2, small[:, 0:1], 2.0, None, ALU.mult))
            link(V.tensor_scalar(nlr, col(LAM_R), -1.0, None, ALU.mult))
            link(V.tensor_scalar(nli, col(LAM_I), -1.0, None, ALU.mult))
            link(V.tensor_scalar(nal, a2, col(LAM_R), -1.0, ALU.add, ALU.mult))
            link(V.tensor_scalar(den_r[:], om[:, 0, :], a2, None, ALU.mult))
            link(V.scalar_tensor_tensor(out=den_r[:], in0=om[:, 1, :], scalar=nlr, in1=den_r[:],
                                        op0=ALU.mult, op1=ALU.add))
            link(V.scalar_tensor_tensor(out=den_r[:], in0=om[:, 2, :], scalar=col(LAM_I), in1=den_r[:],
                                        op0=ALU.mult, op1=ALU.add))
            link(V.tensor_scalar(den_i[:], om[:, 2, :], nal, None, ALU.mult))
            link(V.scalar_tensor_tensor(out=den_i[:], in0=om[:, 1, :], scalar=nli, in1=den_i[:],
                                        op0=ALU.mult, op1=ALU.add))
            link(V.tensor_tensor(mag[:], den_r[:], den_r[:], ALU.mult))
            link(V.tensor_tensor(tmp[:], den_i[:], den_i[:], ALU.mult))
            link(V.tensor_tensor(mag[:], mag[:], tmp[:], ALU.add))
            link(V.reciprocal(tmp[:], mag[:]))
            link(V.tensor_tensor(Rr[:], den_r[:], tmp[:], ALU.mult))
            V.scalar_tensor_tensor(out=Ri[:], in0=den_i[:], scalar=-1.0, in1=tmp[:],
                                   op0=ALU.mult, op1=ALU.mult).then_inc(inv_den_ready, 1)

            dve.wait_ge(cauchy_ready, 1)
            link(V.tensor_copy(kk[:].rearrange("p c l e -> p (c l e)"), acc[0][:, 0:KT * 16]))

            def k(a, b, ri):
                return kk[:, :, :, 4 * ri + 2 * a + b]

            dve.wait_ge(tables_in, 80)
            n = [npl[:, ri, :].unsqueeze(2).to_broadcast([P, KT, 2]) for ri in range(2)]
            w = [cm[:, i] for i in range(16)]

            def cmul(o_r, o_i, ar, ai, br, bi):
                link(V.tensor_tensor(w[12], ar, br, ALU.mult))
                link(V.tensor_tensor(w[13], ai, bi, ALU.mult))
                link(V.tensor_tensor(w[14], ar, bi, ALU.mult))
                link(V.tensor_tensor(w[15], ai, br, ALU.mult))
                link(V.tensor_tensor(o_r, w[12], w[13], ALU.subtract))
                link(V.tensor_tensor(o_i, w[14], w[15], ALU.add))

            cmul(w[0], w[1], k(1, 1, 0), k(1, 1, 1), n[0], n[1])
            link(V.tensor_scalar(w[0], w[0], 1.0, None, ALU.add))
            link(V.tensor_tensor(w[2], w[0], w[0], ALU.mult))
            link(V.tensor_tensor(w[3], w[1], w[1], ALU.mult))
            link(V.tensor_tensor(w[2], w[2], w[3], ALU.add))
            link(V.reciprocal(w[3], w[2]))
            link(V.tensor_tensor(w[0], w[0], w[3], ALU.mult))
            link(V.scalar_tensor_tensor(out=w[1], in0=w[1], scalar=-1.0, in1=w[3], op0=ALU.mult, op1=ALU.mult))
            cmul(w[4], w[5], k(0, 1, 0), k(0, 1, 1), k(1, 0, 0), k(1, 0, 1))
            cmul(w[6], w[7], w[4], w[5], n[0], n[1])
            cmul(w[8], w[9], w[6], w[7], w[0], w[1])
            for o, kc, tc in ((at_r, k(0, 0, 0), w[8]), (at_i, k(0, 0, 1), w[9])):
                link(V.tensor_tensor(o[:], kc, tc, ALU.subtract))
                link(V.tensor_scalar(o[:], o[:], 2.0 / D, None, ALU.mult))

            for layer in range(2):
                for c in range(KT):
                    ar, ai = at_r[:, c, layer:layer + 1], at_i[:, c, layer:layer + 1]
                    cj, sj = cosT[:, c, 0:P], sinT[:, c, 0:P]
                    link(V.tensor_scalar(tw[:], sj, ai, None, ALU.mult))
                    link(V.scalar_tensor_tensor(out=A1[:, layer, c, :], in0=cj, scalar=ar, in1=tw[:],
                                                op0=ALU.mult, op1=ALU.add))
                    link(V.tensor_scalar(tw[:], cj, ai, None, ALU.mult))
                    link(V.scalar_tensor_tensor(out=A2[:, layer, c, :], in0=sj, scalar=ar, in1=tw[:],
                                                op0=ALU.mult, op1=ALU.subtract))
            for layer in range(2):
                dve.wait_ge(toeplitz_sum, layer + 1)
                link(V.tensor_copy(toe[:, layer, :], acc[layer + 1][:]))
                link(V.tensor_tensor(toe[:, layer, 0:P], toe[:, layer, 0:P], diag[:, 0, :], ALU.mult))
                V.scalar_tensor_tensor(out=toe[:, layer, 0:P], in0=diag[:, 1, :], scalar=col(D_0 + layer),
                                       in1=toe[:, layer, 0:P], op0=ALU.mult, op1=ALU.add).then_inc(toe_hi, 1)
            for layer in range(2):
                dve.wait_ge(toe_ready, layer + 1)
                link(V.tensor_tensor(TOEl[:, layer, :], toe[:, layer, :], TOEh[:, layer, :].bitcast(F32),
                                     ALU.subtract))

            dve.wait_ge(x_loaded, 16 * (TILES // BLK))
            V.memset(small[:, 15:16], 0.0).then_inc(x_updated, X_UP0)
            for t in range(STATS_AHEAD):
                stats_step(dve, 0, t, t % SLOTS)
                stats_halves_written(dve, 0, t)
                aggregate_step(t % SLOTS)
            for t in range(XT_AHEAD):
                xt_lo_step(dve, 0, t, t)

            def light(stage):
                kind, _ = LIGHT[stage]
                v0 = stage * TILES
                with dve.Fori(0 // SLOTS, TILES // SLOTS) as grp:
                    t = grp * SLOTS
                    for s in range(SLOTS):
                        stats_step(dve, v0, t + s, s, STATS_AHEAD)
                        stats_halves_written(dve, v0, t + s, STATS_AHEAD)
                        xt_lo_step(dve, v0, t + s, s, XT_AHEAD)
                        aggregate_step(s, STATS_AHEAD)
                        if kind == "quant":
                            dve.wait_ge(bias_added, BIAS_BEFORE[stage] + t + s + 1)
                        update_step(dve, v0, t + s, s % 2, 1.0)

            def ffn(stage, first, last, ahead=True):
                v0 = stage * TILES
                k0 = BLOCKS_BEFORE[stage]
                with dve.Fori(first // SLOTS, last // SLOTS) as grp:
                    t = grp * SLOTS
                    for f in range(FT):
                        m = fwidth(f)
                        n_ = (k0 * FT + f) + grp * FT
                        dve.wait_ge(up_ready, n_ + 1)
                        dve.wait_ge(silu_done, n_ + 1)
                        g = G[:m, f % 2, 0:D]
                        V.tensor_tensor(g, front[2 * (f % 2) + 1][:m, :], g, ALU.mult).then_inc(prod_done, 1)
                        if 2 <= f < 6 and ahead:
                            stats_step(dve, v0, t + f - 2, f - 2, STATS_AHEAD)
                            stats_halves_written(dve, v0, t + f - 2, STATS_AHEAD)
                        dve.wait_ge(hid_hi_done, n_ + 1)
                        V.tensor_tensor(Hl[:m, f % 2, :], g, Hh[:m, f % 2, :].bitcast(F32),
                                        ALU.subtract).then_inc(hid_ready, 1)
                        if 2 <= f < 6 and ahead:
                            aggregate_step(f - 2, STATS_AHEAD)
                    for s in range(BLK):
                        if ahead:
                            xt_lo_step(dve, v0, t + s, s, XT_AHEAD)
                    for s in range(BLK):
                        update_step(dve, v0, t + s, s, 0.5)

            for stage in range(3):
                light(stage)
            ffn(3, 0, TILES)
            light(4)
            ffn(5, 0, TILES - BLK)
            ffn(5, TILES - BLK, TILES, ahead=False)

        @block.tensor
        def _(pe):
            T = nc.tensor
            pe.wait_ge(inv_den_ready, 1)
            pe.wait_ge(setup_dve, 1)
            for c in range(KT):
                o = acc[0][:, c * 16:(c + 1) * 16]
                T.matmul(o, Rr[:, c * P:(c + 1) * P], rhs1[:].rearrange("p l e -> p (l e)"), start=True, stop=False)
                last = T.matmul(o, Ri[:, c * P:(c + 1) * P], rhs2[:].rearrange("p l e -> p (l e)"),
                                start=False, stop=True)
            last.then_inc(cauchy_ready, 1)
            pe.wait_ge(setup_dve, TWISTED)
            for layer in range(2):
                for c in range(KT):
                    T.matmul(acc[layer + 1][:], A1[:, layer, c, :], cosT[:, c, :], start=(c == 0), stop=False)
                    last = T.matmul(acc[layer + 1][:], A2[:, layer, c, :], sinT[:, c, :], start=False,
                                    stop=(c == KT - 1))
                last.then_inc(toeplitz_sum, 1)
            for t in range(XT_AHEAD):
                transpose_step(pe, 0, t, t)

            def light(stage):
                kind, layer = LIGHT[stage]
                v0 = stage * TILES
                with pe.Fori(0 // SLOTS, TILES // SLOTS) as grp:
                    t = grp * SLOTS
                    for s in range(SLOTS):
                        v = v0 + t + s
                        pe.wait_ge(xt_ready, v + 1)
                        pe.wait_ge(x_updated, X_UP0 + v - 1)
                        for j in range(KT):
                            if kind == "quant":
                                wh, wl, lo = Qh[:, j, :], Ql[:, j, :], 0
                            else:
                                wh, wl, lo = TOEh[:, layer, 0:D - j * P], TOEl[:, layer, 0:D - j * P], j * P
                            o = acc[s % 2][:, lo:D]
                            xh, xl = XTh[:, j, s, :], XTl[:, j, s, :]
                            T.matmul(o, xh, wh, start=(j == 0), stop=False)
                            T.matmul(o, xh, wl, start=False, stop=False)
                            last = T.matmul(o, xl, wh, start=False, stop=(j == KT - 1))
                        last.then_inc(acc_ready, 1)
                        transpose_step(pe, v0, t + s, s, XT_AHEAD)

            def ffn(stage, first, last_t, ahead=True):
                v0 = stage * TILES
                k0 = BLOCKS_BEFORE[stage]
                with pe.Fori(first // SLOTS, last_t // SLOTS) as grp:
                    t = grp * SLOTS
                    def gate_up(f):
                        m = fwidth(f)
                        for which, w0, done in ((0, GATE0, gate_ready), (1, UP0, up_ready)):
                            o = front[2 * (f % 2) + which][:m, :]
                            for j in range(KT):
                                cols = slice(w0 + j * F + f * P, w0 + j * F + f * P + m)
                                xh = XTh[:, j, :, :].rearrange("p s r -> p (s r)")
                                xl = XTl[:, j, :, :].rearrange("p s r -> p (s r)")
                                T.matmul(o, Wh[:, cols], xh, start=(j == 0), stop=False)
                                T.matmul(o, Wh[:, cols], xl, start=False, stop=False)
                                last = T.matmul(o, Wl[:, cols], xh, start=False, stop=(j == KT - 1))
                            last.then_inc(done, 1)

                    def down(f):
                        m = fwidth(f)
                        cols = slice(DOWN0 + f * D, DOWN0 + (f + 1) * D)
                        pe.wait_ge(hid_ready, (k0 * FT + f + 1) + grp * FT)
                        if f == 0:
                            pe.wait_ge(x_updated, X_UP0 + v0 + t)
                        for r in range(BLK):
                            hh, hl = Hh[:m, f % 2, r * P:(r + 1) * P], Hl[:m, f % 2, r * P:(r + 1) * P]
                            T.matmul(acc[r][:], hh, Wh[:m, cols], start=(f == 0), stop=False)
                            T.matmul(acc[r][:], hh, Wl[:m, cols], start=False, stop=False)
                            last = T.matmul(acc[r][:], hl, Wh[:m, cols], start=False, stop=(f == FT - 1))
                            if f == FT - 1:
                                last.then_inc(acc_ready, 1)
                        if f < FT - 1:
                            last.then_inc(down_done, 1)

                    for f in range(FT):
                        if f == 0:
                            pe.wait_ge(xt_ready, v0 + t + BLK)
                            if stage == 3:
                                pe.wait_ge(chunk_split, NCHUNK)
                        if f >= 2:
                            pe.wait_ge(prod_done, (k0 * FT + f - 1) + grp * FT)
                        gate_up(f)
                        if f > 0:
                            down(f - 1)
                    if ahead:
                        pe.wait_ge(prod_done, (k0 * FT + FT) + grp * FT)
                        for s in range(BLK):
                            transpose_step(pe, v0, t + s, s, XT_AHEAD)
                    down(FT - 1)

            for stage in range(3):
                light(stage)
            ffn(3, 0, TILES)
            light(4)
            ffn(5, 0, TILES - BLK)
            ffn(5, TILES - BLK, TILES, ahead=False)


TWISTED = 4 + 4 + 8 + 2 + 8 + 14 + 1 + 24 + 7 + 4 + 32


def constants():
    om = np.arange(D)
    ang = 2 * np.pi * ((om[:, None] * om[None, :]) % D) / D
    cos = np.cos(ang).reshape(KT, P, D).transpose(1, 0, 2)
    sin = np.sin(ang).reshape(KT, P, D).transpose(1, 0, 2)
    th = 2 * np.pi * om / D
    wr, wi = np.cos(th), -np.sin(th)
    wi[D // 2] = 0.0
    one_plus = np.stack([1 + wr, wi]).reshape(2, KT, P).transpose(2, 0, 1)
    j, d = np.arange(P)[:, None], np.arange(P)[None, :]
    diag = np.stack([(d >= j), (d == j)], axis=1)
    f = lambda a: np.ascontiguousarray(a, dtype=np.float32)
    return {
        "cos_in": f(cos), "sin_in": f(sin), "omega_in": f(np.stack([1 - wr, 1 + wr, wi])),
        "one_plus_in": f(one_plus), "diag_in": f(diag),
        "qshift": np.tile(np.array([0, 6, 0, 0], np.int32), P // 4).reshape(P, 1),
    }


def layout(inp):
    a = {n: np.asarray(v) for n, v in inp.items()}
    rows = []
    for layer in ("L0", "L1"):
        g = lambda n: a[f"{layer}_attn_{n}"]
        col = lambda v: np.broadcast_to(v.reshape(-1, 1), (NS, 1))
        rows.append(np.concatenate([
            g("Lambda_ri"), g("p_ri"), g("q_ri"), g("Ct_ri").reshape(NS, 2), col(g("log_step")),
            col(a["L0_attn_D"]), col(a["L1_attn_D"]), col(np.zeros(1, np.float32)),
            g("Vc_ri").transpose(0, 2, 1).reshape(NS, 2 * NS),
            np.broadcast_to(g("Bp").reshape(1, NS), (NS, NS))], axis=1))
    k = np.arange(D)
    q = a["L0_ffn_qweight"].T[3 * (k // 4) + np.array([0, 0, 1, 2])[k % 4]]
    tiles = lambda w: w.reshape(KT, P, -1).transpose(1, 0, 2).reshape(P, -1)
    down = np.zeros((FT * P, D), np.float32)
    down[:F] = a["L1_ffn_W_down"].T
    down = down.reshape(FT, P, D).transpose(1, 0, 2).reshape(P, FT * D)
    wffn = np.concatenate([tiles(a["L1_ffn_W_gate"].T), tiles(a["L1_ffn_W_up"].T), down], axis=1)
    c = np.ascontiguousarray
    return {
        "x_in": c(a["L0_attn_u"]), "params": c(np.concatenate(rows, axis=0)),
        "qweight": c(q.reshape(KT, P, D).transpose(1, 0, 2)),
        "qscale": c(a["L0_ffn_weight_scale"].reshape(D)), "qzero": c(a["L0_ffn_weight_zero_point"].reshape(D)),
        "qbias": c(a["L0_ffn_bias"]), "wffn": c(wffn),
    } | constants()


_INS = ["x_in", "params", "qweight", "qshift", "qscale", "qzero", "qbias", "wffn",
        "cos_in", "sin_in", "omega_in", "one_plus_in", "diag_in"]


def kernel(**inputs):
    import concourse.bacc as _bacc
    from concourse.bass_utils import run_bass_kernel_spmd as _run

    nc = _bacc.Bacc("TRN2", target_bir_lowering=False, num_devices=1)
    arrays = layout(inputs)
    args = [nc.dram_tensor(n, arrays[n].shape, mybir.dt.from_np(arrays[n].dtype), kind="ExternalInput").ap()
            for n in _INS]
    args.append(nc.dram_tensor("out", (1, ROWS, D), F32, kind="ExternalOutput").ap())
    build(nc, *args)
    r = _run(nc, [arrays], core_ids=[0])
    return r.results[0]["out"]
```

```python
from contextlib import ExitStack

import numpy as np
import concourse.bass as bass
from concourse import mybir

F32 = mybir.dt.float32
F32R = mybir.dt.float32r
I32 = mybir.dt.int32
ALU = mybir.AluOpType
ACT = mybir.ActivationFunctionType
AX = mybir.AxisListType

P = 128
ROWS = 2048
D = 512
F = 1376
NS = 64
EPS = 1e-5
TILES = ROWS // P
KT = D // P
FT = (F + P - 1) // P
BLK = 4
STATS_AHEAD, RSTD_AHEAD, NORM_AHEAD, XT_AHEAD = 7, 6, 5, 4
SLOTS = 4

GATE0, UP0, DOWN0 = 0, KT * F, 2 * KT * F
WCOLS = DOWN0 + FT * D
CHUNK = 520
NCHUNK = WCOLS // CHUNK
EARLY_CHUNKS = 28
assert NCHUNK * CHUNK == WCOLS
LATE_F = (EARLY_CHUNKS * CHUNK - DOWN0) // D

HALF = KT // 2

(LAM_R, LAM_I, P_R, P_I, Q_R, Q_I, CT_R, CT_I, LOGSTEP, D_0, D_1) = range(11)
VC0 = 12
BP0 = VC0 + 2 * NS
IDENT, CAUSAL, TWIST_C1, TWIST_S, TWIST_C2 = 0, P, 2 * P, 4 * P, 6 * P
NPLUS = 8 * P
FOLD = NPLUS + 2 * KT
TABCOLS = FOLD + HALF
PARCOLS = BP0 + NS


def fwidth(f):
    return min(P, F - f * P)


def build(nc, x_in, params, qweight, qshift, qrows, qbias, wffn, cos_in, sin_in, omega_in, table_in, out):
    with ExitStack() as ctx:
        cursor = [(nc.sbuf_base + 31) // 32 * 32]
        counter = [0]

        def sb(name, shape, dt):
            size = int(np.prod(shape[1:])) * 4
            t = nc.alloc_sbuf_tensor_at(name, shape, dt, offset=cursor[0])
            at = cursor[0]
            cursor[0] += (size + 31) // 32 * 32
            return t, at

        def overlay(name, shape, dt, at):
            return nc.alloc_sbuf_tensor_at(name, shape, dt, offset=at)

        def sem(name):
            return ctx.enter_context(nc.semaphore(name))

        Wh, wh_at = sb("ffn_w_hi", [P, WCOLS], F32R)
        Wl, wl_at = sb("ffn_w_lo", [P, WCOLS], F32R)
        X, _ = sb("x_rows", [P, TILES, D], F32)
        TOEh, _ = sb("toeplitz_hi", [P, 2, D], F32R)
        TOEl, _ = sb("toeplitz_lo", [P, 2, D], F32R)
        XTh, _ = sb("xt_hi", [P, KT, SLOTS, P], F32R)
        XTl, _ = sb("xt_lo", [P, KT, SLOTS, P], F32R)
        LN, _ = sb("normalised", [P, SLOTS, D], F32)
        Hh, h_at = sb("hidden_hi", [P, 2, D], F32R)
        Hl, _ = sb("hidden_lo", [P, 2, D], F32R)
        G, _ = sb("gated", [P, 2, CHUNK], F32)
        ident, _ = sb("identity", [P, P], F32)
        bnst, _ = sb("bn_stats", [P, SLOTS, 6], F32)
        mv, _ = sb("mean_var", [P, SLOTS, 2], F32)
        veps, _ = sb("var_eps", [P, SLOTS, 1], F32)
        rstd, _ = sb("rstd", [P, SLOTS, 1], F32)
        nmr, _ = sb("minus_mean_rstd", [P, SLOTS, 1], F32)
        mr, _ = sb("mean_rstd", [P, SLOTS, 1], F32)
        consts, _ = sb("constant_columns", [P, 5], F32)
        assert cursor[0] <= nc.sbuf_usable_end, (cursor[0], nc.sbuf_usable_end)

        tail = EARLY_CHUNKS * CHUNK * 4
        Qh = overlay("dequant_hi", [P, KT, D], F32R, h_at)
        Ql = overlay("dequant_lo", [P, KT, D], F32R, wl_at + tail)
        biasB = overlay("half_bias", [P, D], F32, wh_at + tail)

        sc = [wh_at]

        def scratch(name, shape, dt=F32):
            t = overlay(name, shape, dt, sc[0])
            sc[0] += (int(np.prod(shape[1:])) * 4 + 31) // 32 * 32
            return t

        par = scratch("s4_params", [P, PARCOLS])
        cosT = scratch("cos_table", [P, HALF, D])
        sinT = scratch("sin_table", [P, HALF, D])
        om = scratch("omega_terms", [P, 3, D])
        tab = scratch("small_tables", [P, TABCOLS])
        qraw = scratch("q_raw", [P, KT, D], I32)
        qsh = scratch("q_shift", [P, 1], I32)
        wq = scratch("dequant_f32", [P, KT, D])
        assert sc[0] <= wh_at + tail
        sc[0] = wl_at
        zsB = scratch("zero_point_and_scale_rows", [P, 2, D])
        den_r = scratch("den_r", [P, D])
        den_i = scratch("den_i", [P, D])
        mag = scratch("den_abs2", [P, D])
        tmp = scratch("den_tmp", [P, D])
        Rr = scratch("inv_den_r", [P, D])
        Ri = scratch("inv_den_i", [P, D])
        bprod = scratch("b_products", [P, 2, NS])
        vec = scratch("b_and_p", [P, 2, 2])
        part = scratch("numer_parts", [P, 4, 2])
        small = scratch("s4_small", [P, 16])
        num_r = scratch("numer_r", [P, 2, 2])
        num_i = scratch("numer_i", [P, 2, 2])
        rhs1 = scratch("cauchy_rhs_re", [P, 2, 8])
        rhs2 = scratch("cauchy_rhs_im", [P, 2, 8])
        kk = scratch("cauchy_sums", [P, KT, 2, 8])
        cm = scratch("complex_work", [P, 16, KT, 2])
        at_r = scratch("at_roots_r", [P, KT, 2])
        at_i = scratch("at_roots_i", [P, KT, 2])
        fold = scratch("folded_roots", [P, 6, HALF, 2])
        tw = scratch("twist_tmp", [P, 2, P])
        A1 = scratch("twisted_1", [P, 2, HALF, P])
        A2 = scratch("twisted_2", [P, 2, HALF, P])
        toe = scratch("toeplitz_f32", [P, 2, D])
        assert sc[0] <= wl_at + tail

        front = [ctx.enter_context(nc.psum_tensor(f"front{i}", [P, D], F32)) for i in range(4)]
        acc = [ctx.enter_context(nc.psum_tensor(f"acc{i}", [P, D], F32)) for i in range(BLK)]

        params_in = sem("params_in")
        omega_in_sem = sem("omega_in")
        quant_in = [sem("quant_in_0"), sem("quant_in_1")]
        rows_in = sem("zero_point_scale_in")
        bias_in = sem("bias_in")
        ident_in = sem("ident_in")
        tables_in = sem("tables_in")
        waves_in = sem("cos_sin_in")
        x_in_sem = [sem(f"x_in_{g}") for g in range(TILES // BLK)]
        chunk_in = [sem("chunk_in_even"), sem("chunk_in_odd")]
        chunk_hi = sem("chunk_hi")
        split_by_pool = sem("split_by_pool")
        split_by_dve = sem("split_by_dve")
        setup_dve = sem("setup_dve")
        setup_pool = sem("setup_pool")
        b_ready = sem("b_ready")
        numer_ready = sem("numer_ready")
        coef_ready = sem("coef_ready")
        den_scaled = sem("den_scaled")
        den_ready = sem("den_ready")
        den_squared = sem("den_squared")
        inv_den_ready = sem("inv_den_ready")
        cauchy_ready = sem("cauchy_ready")
        twisted_ready = sem("twisted_ready")
        toeplitz_sum = sem("toeplitz_sum")
        toe_ready = sem("toe_ready")
        toe_hi = sem("toe_hi")
        toe_split = sem("toe_split")
        dequant_ready = sem("dequant_ready")
        dequant_hi = sem("dequant_hi")
        dequant_split = sem("dequant_split")
        bias_ready = sem("bias_ready")
        const_ready = sem("const_ready")
        stats_raw = sem("stats_raw")
        stats_ready = sem("stats_ready")
        eps_added = sem("eps_added")
        rstd_made = sem("rstd_made")
        mr_made = sem("mr_made")
        rstd_ready = sem("rstd_ready")
        norm_done = sem("norm_done")
        transposed = sem("transposed")
        xt_hi_done = sem("xt_hi_done")
        xt_ready = sem("xt_ready")
        bias_added = sem("bias_added")
        acc_ready = sem("acc_ready")
        x_updated = sem("x_updated")
        gate_ready = sem("gate_ready")
        up_ready = sem("up_ready")
        silu_done = sem("silu_done")
        prod_done = sem("prod_done")
        hid_hi_done = sem("hid_hi_done")
        hid_ready = sem("hid_ready")
        down_done = sem("down_done")
        stored = sem("stored")

        block = ctx.enter_context(nc.Block())

        x_v = x_in.rearrange("o (t p) d -> p (o t) d", p=P)
        out_v = out.rearrange("o (t p) d -> p (o t) d", p=P)

        LIGHT = {0: ("quant", 0), 1: ("conv", 0), 2: ("quant", 0), 4: ("conv", 1)}
        POOL_CHUNKS = TILES
        CHUNK0 = {1: 0, 2: POOL_CHUNKS}
        STAGE2_CHUNKS = EARLY_CHUNKS - POOL_CHUNKS
        BLOCKS_BEFORE = {3: 0, 5: TILES // BLK}
        BIAS_BEFORE = {0: 0, 2: TILES}


        def x_tile(t, ahead=0):
            if isinstance(t, int):
                at = (t + ahead) % TILES
                return X[:, at:at + 1, :].rearrange("p o d -> p (o d)")
            return X[:, bass.ds((t + ahead) % TILES if ahead else t, 1), :].rearrange("p o d -> p (o d)")

        def stats_step(dve, v0, t, s, ahead=0):
            slot = (s + ahead) % SLOTS
            v = v0 + t + ahead
            if v0 or v >= TILES:
                dve.wait_ge(x_updated, v - TILES + 1)
            elif t % BLK == 0 or ahead:
                dve.wait_ge(x_in_sem[v // BLK], 16)
            if v0 or v >= SLOTS:
                dve.wait_ge(norm_done, v - SLOTS + 1)
            nc.vector.bn_stats(bnst[:, slot, :], x_tile(t, ahead)).then_inc(stats_raw, 1)

        def stats_halves_written(dve, v0, t, ahead=0):
            dve.wait_ge(stats_raw, v0 + t + ahead + 1)

        def aggregate_step(s, ahead=0):
            slot = (s + ahead) % SLOTS
            nc.vector.bn_aggr(mv[:, slot, :], bnst[:, slot, :]).then_inc(stats_ready, 1)

        def rstd_step(pool, v0, t, s, ahead=0):
            slot = (s + ahead) % SLOTS
            v = v0 + t + ahead
            pool.wait_ge(stats_ready, v + 1)
            nc.gpsimd.tensor_tensor(veps[:, slot, :], mv[:, slot, 1:2], consts[:, 0:1], ALU.add).then_inc(eps_added, 1)
            pool.wait_ge(eps_added, v + 1)
            nc.gpsimd.tensor_tensor(rstd[:, slot, :], veps[:, slot, :], consts[:, 1:2], ALU.pow).then_inc(rstd_made, 1)
            pool.wait_ge(rstd_made, v + 1)
            nc.gpsimd.tensor_tensor(mr[:, slot, :], mv[:, slot, 0:1], rstd[:, slot, :], ALU.mult).then_inc(mr_made, 1)
            pool.wait_ge(mr_made, v + 1)
            nc.gpsimd.tensor_tensor(nmr[:, slot, :], mr[:, slot, :], consts[:, 2:3], ALU.mult).then_inc(rstd_ready, 1)

        def norm_step(act, v0, t, s, ahead=0):
            slot = (s + ahead) % SLOTS
            v = v0 + t + ahead
            if v0 or v >= SLOTS:
                act.wait_ge(transposed, v - SLOTS + 1)
            act.wait_ge(rstd_ready, v + 1)
            nc.scalar.activation(LN[:, slot, :], x_tile(t, ahead), ACT.Identity, bias=nmr[:, slot, :],
                                 scale=rstd[:, slot, :]).then_inc(norm_done, 1)

        def transpose_step(pe, v0, t, s, ahead=0):
            slot = (s + ahead) % SLOTS
            pe.wait_ge(norm_done, v0 + t + ahead + 1)
            for j in range(KT):
                last = nc.tensor.transpose(front[slot][:, j * P:(j + 1) * P],
                                           LN[:, slot, j * P:(j + 1) * P], ident[:])
            last.then_inc(transposed, 1)

        def bank(slot):
            return front[slot][:, :].rearrange("p (j r) -> p j r", j=KT)

        def xt_hi_step(act, v0, t, s, ahead=0):
            slot = (s + ahead) % SLOTS
            act.wait_ge(transposed, v0 + t + ahead + 1)
            nc.scalar.activation(XTh[:, :, slot, :], bank(slot), ACT.Copy).then_inc(xt_hi_done, 1)

        def xt_lo_step(dve, v0, t, s, ahead=0):
            slot = (s + ahead) % SLOTS
            dve.wait_ge(xt_hi_done, v0 + t + ahead + 1)
            nc.vector.tensor_tensor(XTl[:, :, slot, :], bank(slot), XTh[:, :, slot, :].bitcast(F32),
                                    ALU.subtract).then_inc(xt_ready, 1)

        def update_step(dve, v0, t, a, scale):
            dve.wait_ge(acc_ready, v0 + t + 1)
            xt = x_tile(t)
            if scale == 1.0:
                nc.vector.tensor_tensor(xt, acc[a][:], xt, ALU.add).then_inc(x_updated, 1)
            else:
                nc.vector.scalar_tensor_tensor(out=xt, in0=acc[a][:], scalar=scale, in1=xt,
                                               op0=ALU.mult, op1=ALU.add).then_inc(x_updated, 1)

        @block.sync
        def _(sp):
            sp.dma_start(par[:], params).then_inc(params_in, 16)
            sp.dma_start(X[:, 0:BLK, :], x_v[:, 0:BLK, :]).then_inc(x_in_sem[0], 16)
            sp.dma_start(ident[:], table_in[:, IDENT:IDENT + P]).then_inc(ident_in, 16)
            sp.dma_start(qsh[:], qshift).then_inc(rows_in, 16)
            sp.dma_start(zsB[:], qrows.partition_broadcast(P)).then_inc(rows_in, 16)
            for h in range(HALF):
                js = slice(2 * h, 2 * h + 2)
                sp.dma_start(qraw[:, js, :], qweight[:, js, :]).then_inc(quant_in[h], 16)
            sp.dma_start(om[:], omega_in.partition_broadcast(P)).then_inc(omega_in_sem, 16)
            sp.dma_start(X[:, BLK:2 * BLK, :], x_v[:, BLK:2 * BLK, :]).then_inc(x_in_sem[1], 16)
            sp.dma_start(biasB[:], qbias.partition_broadcast(P)).then_inc(bias_in, 16)
            sp.dma_start(tab[:], table_in).then_inc(tables_in, 16)
            sp.dma_start(X[:, 2 * BLK:3 * BLK, :], x_v[:, 2 * BLK:3 * BLK, :]).then_inc(x_in_sem[2], 16)
            sp.dma_start(cosT[:], cos_in).then_inc(waves_in, 16)
            sp.dma_start(sinT[:], sin_in).then_inc(waves_in, 16)
            sp.dma_start(X[:, 3 * BLK:4 * BLK, :], x_v[:, 3 * BLK:4 * BLK, :]).then_inc(x_in_sem[3], 16)

            def load_chunk(c, parity):
                cols = bass.ds(c * CHUNK, CHUNK)
                sp.dma_start(G[:, parity, :], wffn[:, cols]).then_inc(chunk_in[parity], 16)

            load_chunk(0, 0)
            load_chunk(1, 1)
            with sp.Fori(1, POOL_CHUNKS // 2 + 1) as pair:
                for parity in range(2):
                    sp.wait_ge(split_by_pool, pair * 2 + parity - 1)
                    load_chunk(pair * 2 + parity, parity)
            with sp.Fori(1, (NCHUNK - POOL_CHUNKS) // 2) as pair:
                for parity in range(2):
                    sp.wait_ge(split_by_dve, pair * 2 + parity - 1)
                    load_chunk(POOL_CHUNKS + pair * 2 + parity, parity)
            for b in range(TILES // BLK - 1):
                sp.wait_ge(x_updated, 5 * TILES + (b + 1) * BLK)
                sp.dma_start(out_v[:, b * BLK:(b + 1) * BLK, :], X[:, b * BLK:(b + 1) * BLK, :]).then_inc(stored, 16)
            for t in range(TILES - BLK, TILES):
                sp.wait_ge(x_updated, 5 * TILES + t + 1)
                sp.dma_start(out_v[:, t:t + 1, :], X[:, t:t + 1, :]).then_inc(stored, 16)
            sp.wait_ge(stored, 16 * (TILES // BLK - 1 + BLK))

        @block.gpsimd
        def _(pool):
            TT = nc.gpsimd.tensor_tensor
            values = (EPS, -0.5, -1.0, float(np.e), 2.0)
            for i, value in enumerate(values):
                nc.gpsimd.memset(consts[:, i:i + 1], value).then_inc(const_ready, 1)
            nc.gpsimd.memset(rhs1[:], 0.0).then_inc(const_ready, 1)
            nc.gpsimd.memset(rhs2[:], 0.0).then_inc(const_ready, 1)
            pool.wait_ge(const_ready, len(values) + 2)
            minus, euler, two = consts[:, 2:3], consts[:, 3:4], consts[:, 4:5]

            chain = [0]

            def link(ins):
                chain[0] += 1
                ins.then_inc(setup_pool, 1)
                pool.wait_ge(setup_pool, chain[0])

            def col(c):
                return par[:, c:c + 1]

            pool.wait_ge(params_in, 16)
            a2, nlr, nli, nal, inv, neg = (small[:, i:i + 1] for i in (1, 2, 3, 8, 9, 10))
            TT(nlr, col(LAM_R), minus, ALU.mult)
            TT(nli, col(LAM_I), minus, ALU.mult)
            link(TT(neg, col(LOGSTEP), minus, ALU.mult))
            link(TT(inv, euler, neg, ALU.pow))
            link(TT(a2, inv, two, ALU.mult))
            link(TT(inv, a2, col(LAM_R), ALU.add))
            TT(nal, inv, minus, ALU.mult).then_inc(coef_ready, 1)

            for t in range(SLOTS):
                rstd_step(pool, 0, t, t)

            pool.wait_ge(b_ready, 1)
            for a, (ur, ui) in enumerate(((CT_R, CT_I), (Q_R, Q_I))):
                wide = lambda c: col(c).to_broadcast([P, 2])
                TT(part[:, 0, :], vec[:, 0, :], wide(ur), ALU.mult)
                TT(part[:, 1, :], vec[:, 1, :], wide(ui), ALU.mult)
                TT(part[:, 2, :], vec[:, 1, :], wide(ur), ALU.mult)
                link(TT(part[:, 3, :], vec[:, 0, :], wide(ui), ALU.mult))
                TT(num_r[:, a, :], part[:, 0, :], part[:, 1, :], ALU.add)
                link(TT(num_i[:, a, :], part[:, 2, :], part[:, 3, :], ALU.subtract))
            for layer in range(2):
                rows = slice(layer * NS, layer * NS + NS)
                nr = num_r[rows, :, :].rearrange("p a b -> p (a b)")
                ni = num_i[rows, :, :].rearrange("p a b -> p (a b)")
                nc.gpsimd.tensor_copy(rhs1[rows, layer, 0:4], nr).then_inc(numer_ready, 1)
                nc.gpsimd.tensor_copy(rhs1[rows, layer, 4:8], ni).then_inc(numer_ready, 1)
                TT(rhs2[rows, layer, 0:4], ni, minus[rows, :].to_broadcast([NS, 4]), ALU.mult).then_inc(numer_ready, 1)
                nc.gpsimd.tensor_copy(rhs2[rows, layer, 4:8], nr).then_inc(numer_ready, 1)
                pool.wait_ge(numer_ready, (layer + 1) * 4)

            for t in range(SLOTS, RSTD_AHEAD):
                rstd_step(pool, 0, t, t % SLOTS)

            def bias_step(v0, t):
                pool.wait_ge(norm_done, v0 + t + 1)
                nc.gpsimd.tensor_tensor(x_tile(t), x_tile(t), biasB[:], ALU.add).then_inc(bias_added, 1)

            def chunk_lo_step(c, parity):
                pool.wait_ge(chunk_hi, c + 1)
                cols = bass.ds(c * CHUNK, CHUNK)
                nc.gpsimd.tensor_tensor(Wl[:, cols], G[:, parity, :], Wh[:, cols].bitcast(F32),
                                        ALU.subtract).then_inc(split_by_pool, 1)

            pool.wait_ge(bias_ready, 1)
            for t in range(TILES):
                bias_step(0, t)
                rstd_step(pool, 0, t, t % SLOTS, RSTD_AHEAD)

            def light(stage):
                kind, _ = LIGHT[stage]
                v0 = stage * TILES
                with pool.Fori(0, TILES // SLOTS) as grp:
                    t = grp * SLOTS
                    for s in range(SLOTS):
                        if kind == "quant":
                            bias_step(v0, t + s)
                        rstd_step(pool, v0, t + s, s, RSTD_AHEAD)
                        if stage == 1:
                            pool.wait_ge(toe_split, 2)
                            chunk_lo_step(CHUNK0[stage] + t + s, s % 2)

            light(1)
            light(2)

            def ffn(stage, first, last):
                v0 = stage * TILES
                with pool.Fori(first // SLOTS, last // SLOTS) as grp:
                    t = grp * SLOTS
                    for s in range(BLK):
                        rstd_step(pool, v0, t + s, s, RSTD_AHEAD)

            ffn(3, 0, TILES)
            light(4)
            ffn(5, 0, TILES - BLK)

        @block.scalar
        def _(act):
            def chunk_hi_step(c, parity):
                act.wait_ge(chunk_in[parity], 16 * (c // 2 + 1) if isinstance(c, int) else c * 8 + 16 - 8 * parity)
                cols = bass.ds(c * CHUNK, CHUNK)
                nc.scalar.activation(Wh[:, cols], G[:, parity, :], ACT.Copy).then_inc(chunk_hi, 1)

            def den_scale():
                act.wait_ge(coef_ready, 1)
                act.wait_ge(omega_in_sem, 16)
                nc.scalar.activation(den_r[:], om[:, 0, :], ACT.Copy, scale=small[:, 1:2]).then_inc(den_scaled, 1)
                nc.scalar.activation(den_i[:], om[:, 2, :], ACT.Copy, scale=small[:, 8:9]).then_inc(den_scaled, 1)

            def den_square():
                act.wait_ge(den_ready, 1)
                nc.scalar.activation(mag[:], den_r[:], ACT.Square).then_inc(den_squared, 1)
                nc.scalar.activation(tmp[:], den_i[:], ACT.Square).then_inc(den_squared, 1)

            def toe_round(layer):
                act.wait_ge(toe_ready, layer + 1)
                nc.scalar.activation(TOEh[:, layer, :], toe[:, layer, :], ACT.Copy).then_inc(toe_hi, 1)

            def dequant_round(j):
                act.wait_ge(dequant_ready, j + 1)
                nc.scalar.activation(Qh[:, j, :], wq[:, j, :], ACT.Copy).then_inc(dequant_hi, 1)

            norm_step(act, 0, 0, 0)
            norm_step(act, 0, 1, 1)
            for j in range(KT):
                dequant_round(j)
                xt_hi_step(act, 0, j, j)
                if j < 2:
                    norm_step(act, 0, j + 2, j + 2)
            norm_step(act, 0, SLOTS, 0)
            den_scale()

            def visit(v0, t, s):
                act.wait_ge(acc_ready, v0 + t + 1)
                xt_hi_step(act, v0, t, s, XT_AHEAD)
                norm_step(act, v0, t, s, NORM_AHEAD)

            for t in range(TILES):
                visit(0, t, t % SLOTS)
                if t == 0:
                    den_square()
                if t in (12, 14):
                    toe_round((t - 12) // 2)

            def light(stage, first, last, chunks):
                v0 = stage * TILES
                with act.Fori(first // SLOTS, last // SLOTS) as grp:
                    t = grp * SLOTS
                    for s in range(SLOTS):
                        visit(v0, t + s, s)
                        if chunks:
                            if stage == 1:
                                act.wait_ge(toe_split, 2)
                            chunk_hi_step(CHUNK0[stage] + t + s, s % 2)

            light(1, 0, TILES, True)
            light(2, 0, STAGE2_CHUNKS, True)
            light(2, STAGE2_CHUNKS, TILES, False)
            act.wait_ge(acc_ready, 3 * TILES)
            act.wait_ge(bias_added, 2 * TILES)
            for c in range(EARLY_CHUNKS, NCHUNK):
                chunk_hi_step(c, c % 2)

            def ffn(stage, first, last, ahead=True):
                v0 = stage * TILES
                k0 = BLOCKS_BEFORE[stage]
                with act.Fori(first // SLOTS, last // SLOTS) as grp:
                    t = grp * SLOTS
                    for f in range(FT):
                        m = fwidth(f)
                        n = (k0 * FT + f) + grp * FT
                        act.wait_ge(gate_ready, n + 1)
                        if stage == 3:
                            if f < 2:
                                act.wait_ge(split_by_dve, NCHUNK - POOL_CHUNKS)
                        if stage != 3 or f >= 2:
                            act.wait_ge(hid_ready, n - 1)
                        nc.scalar.activation(G[:m, f % 2, 0:D], front[2 * (f % 2)][:m, :], ACT.Silu
                                             ).then_inc(silu_done, 1)
                        act.wait_ge(prod_done, n + 1)
                        if f == 1:
                            act.wait_ge(acc_ready, v0 + t)
                        elif f >= 2:
                            act.wait_ge(down_done, (FT - 1) * (k0 + grp) + f - 1)
                        elif stage == 5:
                            act.wait_ge(down_done, (FT - 1) * (k0 + grp))
                        nc.scalar.activation(Hh[:m, f % 2, :], G[:m, f % 2, 0:D], ACT.Copy).then_inc(hid_hi_done, 1)
                        if 3 <= f < 6 and ahead:
                            norm_step(act, v0, t + f - 3, f - 3, NORM_AHEAD)
                    for s in range(BLK):
                        if ahead:
                            xt_hi_step(act, v0, t + s, s, XT_AHEAD)
                    if ahead:
                        norm_step(act, v0, t + 3, 3, NORM_AHEAD)

            ffn(3, 0, TILES)
            light(4, 0, TILES, False)
            ffn(5, 0, TILES - BLK)
            ffn(5, TILES - BLK, TILES, ahead=False)

        @block.vector
        def _(dve):
            chain = [0]

            def link(ins):
                chain[0] += 1
                ins.then_inc(setup_dve, 1)
                dve.wait_ge(setup_dve, chain[0])

            V = nc.vector

            def col(c):
                return par[:, c:c + 1]

            nlr, nli = small[:, 2:3], small[:, 3:4]
            dve.wait_ge(params_in, 16)
            vc = par[:, VC0:VC0 + 2 * NS].rearrange("p (c m) -> p c m", c=2)
            bp = par[:, BP0:BP0 + NS].unsqueeze(1).to_broadcast([P, 2, NS])
            V.tensor_copy(vec[:, 0, 1:2], col(P_R))
            V.tensor_copy(vec[:, 1, 1:2], col(P_I))
            link(V.tensor_tensor(bprod[:], vc, bp, ALU.mult))
            V.tensor_reduce(vec[:, :, 0:1], bprod[:], AX.X, ALU.add).then_inc(b_ready, 1)

            for t in range(SLOTS):
                stats_step(dve, 0, t, t)
                stats_halves_written(dve, 0, t)
                aggregate_step(t)

            dve.wait_ge(rows_in, 32)
            link(V.tensor_scalar(zsB[:, 1, :], zsB[:, 1, :], 0.5, None, ALU.mult))

            def dequantise(j):
                dve.wait_ge(quant_in[j // 2], 16)
                link(V.tensor_scalar(qraw[:, j, :], qraw[:, j, :], qsh[:, 0:1], 63,
                                     ALU.logical_shift_right, ALU.bitwise_and))
                link(V.tensor_tensor(wq[:, j, :], qraw[:, j, :], zsB[:, 0, :], ALU.subtract))
                V.tensor_tensor(wq[:, j, :], wq[:, j, :], zsB[:, 1, :], ALU.mult).then_inc(dequant_ready, 1)

            def dequant_lo(j):
                dve.wait_ge(dequant_hi, j + 1)
                V.tensor_tensor(Ql[:, j, :], wq[:, j, :], Qh[:, j, :].bitcast(F32), ALU.subtract
                                ).then_inc(dequant_split, 1)

            dequantise(0)
            for j in range(KT):
                if j < KT - 1:
                    dequantise(j + 1)
                dequant_lo(j)
                xt_lo_step(dve, 0, j, j)
            for t in range(SLOTS, STATS_AHEAD):
                stats_step(dve, 0, t, t % SLOTS)
                stats_halves_written(dve, 0, t)
                aggregate_step(t % SLOTS)
            dve.wait_ge(bias_in, 16)
            V.tensor_scalar(biasB[:], biasB[:], 0.5, None, ALU.mult).then_inc(bias_ready, 1)

            def denominators():
                dve.wait_ge(den_scaled, 2)
                link(V.scalar_tensor_tensor(out=den_r[:], in0=om[:, 1, :], scalar=nlr, in1=den_r[:],
                                            op0=ALU.mult, op1=ALU.add))
                link(V.scalar_tensor_tensor(out=den_r[:], in0=om[:, 2, :], scalar=col(LAM_I), in1=den_r[:],
                                            op0=ALU.mult, op1=ALU.add))
                V.scalar_tensor_tensor(out=den_i[:], in0=om[:, 1, :], scalar=nli, in1=den_i[:],
                                       op0=ALU.mult, op1=ALU.add).then_inc(den_ready, 1)

            def invert(c):
                cols = slice(c * P, (c + 1) * P)
                if c == 0:
                    dve.wait_ge(den_squared, 2)
                link(V.tensor_tensor(mag[:, cols], mag[:, cols], tmp[:, cols], ALU.add))
                link(V.reciprocal(tmp[:, cols], mag[:, cols]))
                V.tensor_tensor(Rr[:, cols], den_r[:, cols], tmp[:, cols], ALU.mult)
                V.scalar_tensor_tensor(out=Ri[:, cols], in0=den_i[:, cols], scalar=-1.0, in1=tmp[:, cols],
                                       op0=ALU.mult, op1=ALU.mult).then_inc(inv_den_ready, 1)

            def k(a, b, ri):
                return kk[:, :, :, 4 * ri + 2 * a + b]

            n = [tab[:, NPLUS + ri * KT:NPLUS + (ri + 1) * KT].unsqueeze(2).to_broadcast([P, KT, 2]) for ri in range(2)]
            w = [cm[:, i] for i in range(16)]

            def cmul(o_r, o_i, ar, ai, br, bi):
                V.tensor_tensor(w[12], ar, br, ALU.mult)
                V.tensor_tensor(w[13], ai, bi, ALU.mult)
                V.tensor_tensor(w[14], ar, bi, ALU.mult)
                link(V.tensor_tensor(w[15], ai, br, ALU.mult))
                V.tensor_tensor(o_r, w[12], w[13], ALU.subtract)
                link(V.tensor_tensor(o_i, w[14], w[15], ALU.add))


            def resolvent():
                dve.wait_ge(cauchy_ready, 1)
                dve.wait_ge(tables_in, 16)
                link(V.tensor_copy(kk[:].rearrange("p c l e -> p (c l e)"), acc[2][:, 0:KT * 16]))
                cmul(w[0], w[1], k(1, 1, 0), k(1, 1, 1), n[0], n[1])
                link(V.tensor_scalar(w[0], w[0], 1.0, None, ALU.add))
                V.tensor_tensor(w[2], w[0], w[0], ALU.mult)
                link(V.tensor_tensor(w[3], w[1], w[1], ALU.mult))
                link(V.tensor_tensor(w[2], w[2], w[3], ALU.add))
                link(V.reciprocal(w[3], w[2]))
                V.tensor_tensor(w[0], w[0], w[3], ALU.mult)
                link(V.scalar_tensor_tensor(out=w[1], in0=w[1], scalar=-1.0, in1=w[3], op0=ALU.mult, op1=ALU.mult))

            def roots():
                cmul(w[4], w[5], k(0, 1, 0), k(0, 1, 1), k(1, 0, 0), k(1, 0, 1))
                cmul(w[6], w[7], w[4], w[5], n[0], n[1])
                cmul(w[8], w[9], w[6], w[7], w[0], w[1])
                V.tensor_tensor(w[10], k(0, 0, 0), w[8], ALU.subtract)
                link(V.tensor_tensor(w[11], k(0, 0, 1), w[9], ALU.subtract))
                V.tensor_scalar(at_r[:], w[10], 2.0 / D, None, ALU.mult)
                link(V.tensor_scalar(at_i[:], w[11], 2.0 / D, None, ALU.mult))

            even, odd = fold[:, 4], fold[:, 5]

            def fold_roots():
                apart = tab[:, FOLD:FOLD + HALF].unsqueeze(2).to_broadcast([P, HALF, 2])
                r, r_, i, i_ = at_r[:, 0:HALF], at_r[:, HALF:KT], at_i[:, 0:HALF], at_i[:, HALF:KT]
                V.tensor_tensor(fold[:, 0], r_, apart, ALU.mult)
                link(V.tensor_tensor(fold[:, 1], i, i_, ALU.subtract))
                V.tensor_tensor(even, r, fold[:, 0], ALU.add)
                V.tensor_tensor(fold[:, 2], fold[:, 1], apart, ALU.mult)
                link(V.tensor_tensor(fold[:, 3], r_, fold[:, 0], ALU.subtract))
                link(V.tensor_tensor(odd, fold[:, 2], fold[:, 3], ALU.add))

            def twist(layer):
                for c in range(HALF):
                    e, o = even[:, c, layer:layer + 1], odd[:, c, layer:layer + 1]
                    c1, sn, c2 = (tab[:, at + c * P:at + (c + 1) * P] for at in (TWIST_C1, TWIST_S, TWIST_C2))
                    V.tensor_scalar(tw[:, 0, :], sn, o, None, ALU.mult)
                    link(V.tensor_scalar(tw[:, 1, :], c2, o, None, ALU.mult))
                    V.scalar_tensor_tensor(out=A1[:, layer, c, :], in0=c1, scalar=e, in1=tw[:, 0, :],
                                           op0=ALU.mult, op1=ALU.add)
                    last = V.scalar_tensor_tensor(out=A2[:, layer, c, :], in0=sn, scalar=e, in1=tw[:, 1, :],
                                                  op0=ALU.mult, op1=ALU.subtract)
                    if c < HALF - 1:
                        link(last)
                last.then_inc(twisted_ready, 1)

            def strip(layer):
                dve.wait_ge(toeplitz_sum, layer + 1)
                link(V.tensor_copy(toe[:, layer, :], acc[3 - layer][:]))
                link(V.tensor_tensor(toe[:, layer, 0:P], toe[:, layer, 0:P], tab[:, CAUSAL:CAUSAL + P], ALU.mult))
                V.scalar_tensor_tensor(out=toe[:, layer, 0:P], in0=tab[:, IDENT:IDENT + P], scalar=col(D_0 + layer),
                                       in1=toe[:, layer, 0:P], op0=ALU.mult, op1=ALU.add).then_inc(toe_ready, 1)

            def strip_lo(layer):
                dve.wait_ge(toe_hi, layer + 1)
                V.tensor_tensor(TOEl[:, layer, :], toe[:, layer, :], TOEh[:, layer, :].bitcast(F32),
                                ALU.subtract).then_inc(toe_split, 1)

            def visit(v0, t, s, biased, a):
                if biased is not None:
                    dve.wait_ge(bias_added, biased)
                update_step(dve, v0, t, a, 1.0)
                stats_step(dve, v0, t, s, STATS_AHEAD)
                stats_halves_written(dve, v0, t, STATS_AHEAD)
                xt_lo_step(dve, v0, t, s, XT_AHEAD)
                aggregate_step(s, STATS_AHEAD)

            for t in range(TILES):
                visit(0, t, t % SLOTS, t + 1, t % 2)
                if t == 0:
                    denominators()
                if t in range(2, 2 + KT):
                    invert(t - 2)
                if t == 7:
                    resolvent()
                if t == 8:
                    roots()
                if t == 9:
                    fold_roots()
                    twist(0)
                if t == 10:
                    twist(1)
                if t in (12, 14):
                    strip((t - 12) // 2)
                if t in (13, 15):
                    strip_lo((t - 13) // 2)

            def chunk_lo_step(c, parity):
                dve.wait_ge(chunk_hi, c + 1)
                cols = bass.ds(c * CHUNK, CHUNK)
                V.tensor_tensor(Wl[:, cols], G[:, parity, :], Wh[:, cols].bitcast(F32),
                                ALU.subtract).then_inc(split_by_dve, 1)

            def light(stage, first, last, chunks):
                kind, _ = LIGHT[stage]
                v0 = stage * TILES
                with dve.Fori(first // SLOTS, last // SLOTS) as grp:
                    t = grp * SLOTS
                    for s in range(SLOTS):
                        visit(v0, t + s, s, BIAS_BEFORE[stage] + t + s + 1 if kind == "quant" else None, s)
                        if chunks:
                            chunk_lo_step(CHUNK0[stage] + t + s, s % 2)

            def ffn(stage, first, last, ahead=True):
                v0 = stage * TILES
                k0 = BLOCKS_BEFORE[stage]
                with dve.Fori(first // SLOTS, last // SLOTS) as grp:
                    t = grp * SLOTS
                    for f in range(FT):
                        m = fwidth(f)
                        n_ = (k0 * FT + f) + grp * FT
                        dve.wait_ge(up_ready, n_ + 1)
                        dve.wait_ge(silu_done, n_ + 1)
                        g = G[:m, f % 2, 0:D]
                        V.tensor_tensor(g, front[2 * (f % 2) + 1][:m, :], g, ALU.mult).then_inc(prod_done, 1)
                        if 2 <= f < 6 and ahead:
                            stats_step(dve, v0, t + f - 2, f - 2, STATS_AHEAD)
                            stats_halves_written(dve, v0, t + f - 2, STATS_AHEAD)
                        dve.wait_ge(hid_hi_done, n_ + 1)
                        V.tensor_tensor(Hl[:m, f % 2, :], g, Hh[:m, f % 2, :].bitcast(F32),
                                        ALU.subtract).then_inc(hid_ready, 1)
                        if 2 <= f < 6 and ahead:
                            aggregate_step(f - 2, STATS_AHEAD)
                    for s in range(BLK):
                        if ahead:
                            xt_lo_step(dve, v0, t + s, s, XT_AHEAD)
                    for s in range(BLK):
                        update_step(dve, v0, t + s, s, 0.5)

            light(1, 0, TILES, False)
            light(2, 0, STAGE2_CHUNKS, True)
            light(2, STAGE2_CHUNKS, TILES, False)
            for c in range(EARLY_CHUNKS, NCHUNK):
                chunk_lo_step(c, c % 2)
            ffn(3, 0, TILES)
            light(4, 0, TILES, False)
            ffn(5, 0, TILES - BLK)
            ffn(5, TILES - BLK, TILES, ahead=False)

        @block.tensor
        def _(pe):
            T = nc.tensor
            pe.wait_ge(ident_in, 16)
            for t in range(XT_AHEAD):
                transpose_step(pe, 0, t, t)

            def products(stage, s, a):
                kind, layer = LIGHT[stage]
                for j in range(KT):
                    if kind == "quant":
                        wh, wl, lo = Qh[:, j, :], Ql[:, j, :], 0
                        if stage == 0:
                            pe.wait_ge(dequant_split, j + 1)
                    else:
                        wh, wl, lo = TOEh[:, layer, 0:D - j * P], TOEl[:, layer, 0:D - j * P], j * P
                    o = acc[a][:, lo:D]
                    xh, xl = XTh[:, j, s, :], XTl[:, j, s, :]
                    T.matmul(o, xh, wh, start=(j == 0), stop=False)
                    T.matmul(o, xh, wl, start=False, stop=False)
                    last = T.matmul(o, xl, wh, start=False, stop=(j == KT - 1))
                last.then_inc(acc_ready, 1)

            def cauchy():
                pe.wait_ge(inv_den_ready, KT)
                pe.wait_ge(numer_ready, 8)
                for c in range(KT):
                    o = acc[2][:, c * 16:(c + 1) * 16]
                    T.matmul(o, Rr[:, c * P:(c + 1) * P], rhs1[:].rearrange("p l e -> p (l e)"), start=True, stop=False)
                    last = T.matmul(o, Ri[:, c * P:(c + 1) * P], rhs2[:].rearrange("p l e -> p (l e)"),
                                    start=False, stop=True)
                last.then_inc(cauchy_ready, 1)

            def toeplitz(layer):
                pe.wait_ge(twisted_ready, layer + 1)
                pe.wait_ge(waves_in, 32)
                for c in range(HALF):
                    T.matmul(acc[3 - layer][:], A1[:, layer, c, :], cosT[:, c, :], start=(c == 0), stop=False)
                    last = T.matmul(acc[3 - layer][:], A2[:, layer, c, :], sinT[:, c, :], start=False,
                                    stop=(c == HALF - 1))
                last.then_inc(toeplitz_sum, 1)

            for t in range(TILES):
                pe.wait_ge(xt_ready, t + 1)
                if t >= 2:
                    pe.wait_ge(x_updated, t - 1)
                products(0, t % SLOTS, t % 2)
                transpose_step(pe, 0, t, t % SLOTS, XT_AHEAD)
                if t == 7:
                    cauchy()
                if t in (11, 13):
                    toeplitz((t - 11) // 2)

            def light(stage):
                v0 = stage * TILES
                if stage == 1:
                    pe.wait_ge(x_updated, TILES)
                with pe.Fori(0, TILES // SLOTS) as grp:
                    t = grp * SLOTS
                    for s in range(SLOTS):
                        v = v0 + t + s
                        pe.wait_ge(xt_ready, v + 1)
                        if stage == 1:
                            pe.wait_ge(toe_split, 2)
                        pe.wait_ge(x_updated, v - SLOTS + 1)
                        products(stage, s, s)
                        transpose_step(pe, v0, t + s, s, XT_AHEAD)

            def ffn(stage, first, last_t, ahead=True):
                v0 = stage * TILES
                k0 = BLOCKS_BEFORE[stage]
                with pe.Fori(first // SLOTS, last_t // SLOTS) as grp:
                    t = grp * SLOTS
                    def gate_up(f):
                        m = fwidth(f)
                        for which, w0, done in ((0, GATE0, gate_ready), (1, UP0, up_ready)):
                            o = front[2 * (f % 2) + which][:m, :]
                            for j in range(KT):
                                cols = slice(w0 + j * F + f * P, w0 + j * F + f * P + m)
                                xh = XTh[:, j, :, :].rearrange("p s r -> p (s r)")
                                xl = XTl[:, j, :, :].rearrange("p s r -> p (s r)")
                                T.matmul(o, Wh[:, cols], xh, start=(j == 0), stop=False)
                                T.matmul(o, Wh[:, cols], xl, start=False, stop=False)
                                last = T.matmul(o, Wl[:, cols], xh, start=False, stop=(j == KT - 1))
                            last.then_inc(done, 1)

                    def down(f):
                        m = fwidth(f)
                        cols = slice(DOWN0 + f * D, DOWN0 + (f + 1) * D)
                        pe.wait_ge(hid_ready, (k0 * FT + f + 1) + grp * FT)
                        if stage == 3 and f == LATE_F:
                            pe.wait_ge(split_by_dve, NCHUNK - POOL_CHUNKS)
                        if f == 0:
                            pe.wait_ge(x_updated, v0 + t)
                        for r in range(BLK):
                            hh, hl = Hh[:m, f % 2, r * P:(r + 1) * P], Hl[:m, f % 2, r * P:(r + 1) * P]
                            T.matmul(acc[r][:], hh, Wh[:m, cols], start=(f == 0), stop=False)
                            T.matmul(acc[r][:], hh, Wl[:m, cols], start=False, stop=False)
                            last = T.matmul(acc[r][:], hl, Wh[:m, cols], start=False, stop=(f == FT - 1))
                            if f == FT - 1:
                                last.then_inc(acc_ready, 1)
                        if f < FT - 1:
                            last.then_inc(down_done, 1)

                    for f in range(FT):
                        if f == 0:
                            pe.wait_ge(xt_ready, v0 + t + BLK)
                            if stage == 3:
                                pe.wait_ge(split_by_pool, POOL_CHUNKS)
                                pe.wait_ge(split_by_dve, EARLY_CHUNKS - POOL_CHUNKS)
                        if f >= 2:
                            pe.wait_ge(prod_done, (k0 * FT + f - 1) + grp * FT)
                        gate_up(f)
                        if f > 0:
                            down(f - 1)
                    if ahead:
                        pe.wait_ge(prod_done, (k0 * FT + FT) + grp * FT)
                        for s in range(BLK):
                            transpose_step(pe, v0, t + s, s, XT_AHEAD)
                    down(FT - 1)

            light(1)
            light(2)
            ffn(3, 0, TILES)
            light(4)
            ffn(5, 0, TILES - BLK)
            ffn(5, TILES - BLK, TILES, ahead=False)


def constants():
    half = D // 2
    w = np.arange(half)
    d = np.arange(D)
    rows = lambda a: a.reshape(-1, P, a.shape[-1]).transpose(1, 0, 2)
    f = lambda a: np.ascontiguousarray(a, dtype=np.float32)
    ang = 2 * np.pi * ((w[:, None] * d[None, :]) % D) / D
    cos, sin = np.cos(ang), np.sin(ang)
    freq = np.concatenate([w, np.concatenate([[half], D - w[1:]])])
    th = 2 * np.pi * freq / D
    wr, wi = np.cos(th), -np.sin(th)
    wi[freq == half] = 0.0
    c1, sn, c2 = cos[:, :P].copy(), sin[:, :P].copy(), cos[:, :P].copy()
    alternate = 1.0 - 2.0 * (d % 2)
    sin[0] = alternate
    c2[0] = -alternate[:P]
    apart = np.ones((half, 1))
    apart[0] = 0.0
    j, e = np.arange(P)[:, None], np.arange(P)[None, :]
    flat = lambda a: rows(a).reshape(P, -1)
    table = np.concatenate([e == j, e >= j, flat(c1), flat(sn), flat(c2),
                            flat((1 + wr)[:, None]), flat(wi[:, None]), flat(apart)], axis=1)
    return {
        "cos_in": f(rows(cos)), "sin_in": f(rows(sin)), "omega_in": f(np.stack([1 - wr, 1 + wr, wi])),
        "table_in": f(table), "qshift": np.tile(np.array([0, 6, 0, 0], np.int32), P // 4).reshape(P, 1),
    }


def layout(inp):
    a = {n: np.asarray(v) for n, v in inp.items()}
    rows = []
    for layer in ("L0", "L1"):
        g = lambda n: a[f"{layer}_attn_{n}"]
        col = lambda v: np.broadcast_to(v.reshape(-1, 1), (NS, 1))
        rows.append(np.concatenate([
            g("Lambda_ri"), g("p_ri"), g("q_ri"), g("Ct_ri").reshape(NS, 2), col(g("log_step")),
            col(a["L0_attn_D"]), col(a["L1_attn_D"]), col(np.zeros(1, np.float32)),
            g("Vc_ri").transpose(0, 2, 1).reshape(NS, 2 * NS),
            np.broadcast_to(g("Bp").reshape(1, NS), (NS, NS))], axis=1))
    k = np.arange(D)
    q = a["L0_ffn_qweight"].T[3 * (k // 4) + np.array([0, 0, 1, 2])[k % 4]]
    tiles = lambda w: w.reshape(KT, P, -1).transpose(1, 0, 2).reshape(P, -1)
    down = np.zeros((FT * P, D), np.float32)
    down[:F] = a["L1_ffn_W_down"].T
    down = down.reshape(FT, P, D).transpose(1, 0, 2).reshape(P, FT * D)
    wffn = np.concatenate([tiles(a["L1_ffn_W_gate"].T), tiles(a["L1_ffn_W_up"].T), down], axis=1)
    c = np.ascontiguousarray
    return {
        "x_in": c(a["L0_attn_u"]), "params": c(np.concatenate(rows, axis=0)),
        "qweight": c(q.reshape(KT, P, D).transpose(1, 0, 2)),
        "qrows": c(np.stack([a["L0_ffn_weight_zero_point"].reshape(D), a["L0_ffn_weight_scale"].reshape(D)])),
        "qbias": c(a["L0_ffn_bias"]), "wffn": c(wffn),
    } | constants()


_INS = ["x_in", "params", "qweight", "qshift", "qrows", "qbias", "wffn", "cos_in", "sin_in", "omega_in", "table_in"]


def kernel(**inputs):
    import concourse.bacc as _bacc
    from concourse.bass_utils import run_bass_kernel_spmd as _run

    nc = _bacc.Bacc("TRN2", target_bir_lowering=False, num_devices=1)
    arrays = layout(inputs)
    args = [nc.dram_tensor(n, arrays[n].shape, mybir.dt.from_np(arrays[n].dtype), kind="ExternalInput").ap()
            for n in _INS]
    args.append(nc.dram_tensor("out", (1, ROWS, D), F32, kind="ExternalOutput").ap())
    build(nc, *args)
    r = _run(nc, [arrays], core_ids=[0])
    return r.results[0]["out"]
```

```python
from contextlib import ExitStack

import numpy as np
import concourse.bass as bass
from concourse import mybir

F32 = mybir.dt.float32
F32R = mybir.dt.float32r
I32 = mybir.dt.int32
ALU = mybir.AluOpType
ACT = mybir.ActivationFunctionType
AX = mybir.AxisListType

P = 128
ROWS = 2048
D = 512
F = 1376
NS = 64
EPS = 1e-5
TILES = ROWS // P
KT = D // P
FT = (F + P - 1) // P
CONST_COLUMNS = 5
BLK = 4
STATS_AHEAD, RSTD_AHEAD, NORM_AHEAD, XT_AHEAD = 7, 6, 5, 4
SLOTS = 4

GATE0, UP0, DOWN0 = 0, KT * F, 2 * KT * F
WCOLS = DOWN0 + FT * D
CHUNK = 520
NCHUNK = WCOLS // CHUNK
EARLY_CHUNKS = 28
assert NCHUNK * CHUNK == WCOLS

HALF = KT // 2

(LAM_R, LAM_I, P_R, P_I, Q_R, Q_I, CT_R, CT_I, LOGSTEP, D_0, D_1) = range(11)
VC0 = 12
BP0 = VC0 + 2 * NS
IDENT, CAUSAL, TWIST_C1, TWIST_S, TWIST_C2 = 0, P, 2 * P, 4 * P, 6 * P
NPLUS = 8 * P
FOLD = NPLUS + 2 * KT
TABCOLS = FOLD + HALF
PARCOLS = BP0 + NS


def chunks_up_to(col):
    return -(-col // CHUNK)


def fwidth(f):
    return min(P, F - f * P)


def build(nc, x_in, params, qweight, qshift, qrows, qbias, wffn, cos_in, sin_in, omega_in, table_in, out):
    with ExitStack() as ctx:
        cursor = [(nc.sbuf_base + 31) // 32 * 32]
        counter = [0]

        def sb(name, shape, dt):
            size = int(np.prod(shape[1:])) * 4
            t = nc.alloc_sbuf_tensor_at(name, shape, dt, offset=cursor[0])
            at = cursor[0]
            cursor[0] += (size + 31) // 32 * 32
            return t, at

        def overlay(name, shape, dt, at):
            return nc.alloc_sbuf_tensor_at(name, shape, dt, offset=at)

        def sem(name):
            return ctx.enter_context(nc.semaphore(name))

        Wh, wh_at = sb("ffn_w_hi", [P, WCOLS], F32R)
        Wl, wl_at = sb("ffn_w_lo", [P, WCOLS], F32R)
        X, _ = sb("x_rows", [P, TILES, D], F32)
        TOEh, _ = sb("toeplitz_hi", [P, 2, D], F32R)
        TOEl, _ = sb("toeplitz_lo", [P, 2, D], F32R)
        XTh, _ = sb("xt_hi", [P, KT, SLOTS, P], F32R)
        XTl, _ = sb("xt_lo", [P, KT, SLOTS, P], F32R)
        LN, _ = sb("normalised", [P, SLOTS, D], F32)
        Hh, h_at = sb("hidden_hi", [P, 2, D], F32R)
        Hl, _ = sb("hidden_lo", [P, 2, D], F32R)
        G, _ = sb("gated", [P, 2, CHUNK], F32)
        ident, _ = sb("identity", [P, P], F32)
        bnst, _ = sb("bn_stats", [P, SLOTS, 6], F32)
        mv, _ = sb("mean_var", [P, SLOTS, 2], F32)
        veps, _ = sb("var_eps", [P, SLOTS, 1], F32)
        rstd, _ = sb("rstd", [P, SLOTS, 1], F32)
        nmr, _ = sb("minus_mean_rstd", [P, SLOTS, 1], F32)
        minus_mean, _ = sb("minus_mean", [P, SLOTS, 1], F32)
        consts, _ = sb("constant_columns", [P, CONST_COLUMNS], F32)
        silu_warm, _ = sb("silu_of_a_constant", [P, 1], F32)
        assert cursor[0] <= nc.sbuf_usable_end, (cursor[0], nc.sbuf_usable_end)

        tail = EARLY_CHUNKS * CHUNK * 4
        Qh = overlay("dequant_hi", [P, KT, D], F32R, h_at)
        Ql = overlay("dequant_lo", [P, KT, D], F32R, wl_at + tail)
        biasB = overlay("half_bias", [P, D], F32, wh_at + tail)

        sc = [wh_at]

        def scratch(name, shape, dt=F32):
            t = overlay(name, shape, dt, sc[0])
            sc[0] += (int(np.prod(shape[1:])) * 4 + 31) // 32 * 32
            return t

        par = scratch("s4_params", [P, PARCOLS])
        cosT = scratch("cos_table", [P, HALF, D])
        sinT = scratch("sin_table", [P, HALF, D])
        om = scratch("omega_terms", [P, 3, D])
        tab = scratch("small_tables", [P, TABCOLS])
        qraw = scratch("q_raw", [P, KT, D], I32)
        qsh = scratch("q_shift", [P, 1], I32)
        wq = scratch("dequant_f32", [P, KT, D])
        assert sc[0] <= wh_at + tail
        sc[0] = wl_at
        zsB = scratch("zero_point_and_scale_rows", [P, 2, D])
        den_r = scratch("den_r", [P, D])
        den_i = scratch("den_i", [P, D])
        mag = scratch("den_abs2", [P, D])
        tmp = scratch("den_tmp", [P, D])
        Rr = scratch("inv_den_r", [P, D])
        Ri = scratch("inv_den_i", [P, D])
        bprod = scratch("b_products", [P, 2, NS])
        vec = scratch("b_and_p", [P, 2, 2])
        part = scratch("numer_parts", [P, 4, 2])
        small = scratch("s4_small", [P, 16])
        num_r = scratch("numer_r", [P, 2, 2])
        num_i = scratch("numer_i", [P, 2, 2])
        rhs1 = scratch("cauchy_rhs_re", [P, 2, 8])
        rhs2 = scratch("cauchy_rhs_im", [P, 2, 8])
        kk = scratch("cauchy_sums", [P, KT, 2, 8])
        cm = scratch("complex_work", [P, 16, KT, 2])
        at_r = scratch("at_roots_r", [P, KT, 2])
        at_i = scratch("at_roots_i", [P, KT, 2])
        fold = scratch("folded_roots", [P, 6, HALF, 2])
        tw = scratch("twist_tmp", [P, 2, P])
        A1 = scratch("twisted_1", [P, 2, HALF, P])
        A2 = scratch("twisted_2", [P, 2, HALF, P])
        toe = scratch("toeplitz_f32", [P, 2, D])
        assert sc[0] <= wl_at + tail

        front = [ctx.enter_context(nc.psum_tensor(f"front{i}", [P, D], F32)) for i in range(4)]
        acc = [ctx.enter_context(nc.psum_tensor(f"acc{i}", [P, D], F32)) for i in range(BLK)]

        params_in = sem("params_in")
        omega_in_sem = sem("omega_in")
        quant_in = [sem(f"quant_in_{j}") for j in range(KT)]
        rows_in = sem("zero_point_scale_in")
        bias_in = sem("bias_in")
        ident_in = sem("ident_in")
        tables_in = sem("tables_in")
        waves_in = sem("cos_sin_in")
        x_first_in = [sem("x_in_tiles_0_1"), sem("x_in_tiles_2_3")]
        x_in_sem = {g: sem(f"x_in_{g}") for g in range(1, TILES // BLK)}
        chunk_in = [sem("chunk_in_even"), sem("chunk_in_odd")]
        chunk_hi = sem("chunk_hi")
        split_by_pool = sem("split_by_pool")
        split_by_dve = sem("split_by_dve")
        setup_dve = sem("setup_dve")
        setup_pool = sem("setup_pool")
        b_ready = sem("b_ready")
        numer_ready = sem("numer_ready")
        coef_ready = sem("coef_ready")
        den_scaled = sem("den_scaled")
        den_ready = sem("den_ready")
        den_squared = sem("den_squared")
        mag_ready = sem("mag_ready")
        den_recip = sem("den_recip")
        inv_den_ready = sem("inv_den_ready")
        cauchy_ready = sem("cauchy_ready")
        twisted_ready = sem("twisted_ready")
        toeplitz_sum = sem("toeplitz_sum")
        toe_ready = sem("toe_ready")
        toe_hi = sem("toe_hi")
        toe_split = sem("toe_split")
        dequant_ready = sem("dequant_ready")
        dequant_hi = sem("dequant_hi")
        dequant_split = sem("dequant_split")
        bias_ready = sem("bias_ready")
        scale_halved = sem("scale_halved")
        const_ready = sem("const_ready")
        stats_raw = sem("stats_raw")
        stats_ready = sem("stats_ready")
        eps_added = sem("eps_added")
        rstd_made = sem("rstd_made")
        mean_negated = sem("mean_negated")
        rstd_ready = sem("rstd_ready")
        norm_done = sem("norm_done")
        transposed = sem("transposed")
        xt_hi_done = sem("xt_hi_done")
        xt_ready = sem("xt_ready")
        bias_added = sem("bias_added")
        acc_ready = sem("acc_ready")
        x_updated = sem("x_updated")
        gate_ready = sem("gate_ready")
        up_ready = sem("up_ready")
        silu_done = sem("silu_done")
        prod_done = sem("prod_done")
        hid_hi_done = sem("hid_hi_done")
        hid_ready = sem("hid_ready")
        down_done = sem("down_done")
        stored = sem("stored")

        block = ctx.enter_context(nc.Block())

        x_v = x_in.rearrange("o (t p) d -> p (o t) d", p=P)
        out_v = out.rearrange("o (t p) d -> p (o t) d", p=P)

        LIGHT = {0: ("quant", 0), 1: ("conv", 0), 2: ("quant", 0), 4: ("conv", 1)}
        POOL_CHUNKS = TILES
        WEIGHT_VISITS = {1: ((0, TILES, 1, 0),),
                         2: ((0, TILES - SLOTS, 1, POOL_CHUNKS), (TILES - SLOTS, TILES, 0, 0))}
        NO_WEIGHTS = (0, TILES, 0, 0)
        BLOCKS_BEFORE = {3: 0, 5: TILES // BLK}
        BIAS_BEFORE = {0: 0, 2: TILES}

        def sum_bank(stage, s):
            return (s + 2) % BLK if stage < 3 else s


        def x_tile(t, ahead=0):
            if isinstance(t, int):
                at = (t + ahead) % TILES
                return X[:, at:at + 1, :].rearrange("p o d -> p (o d)")
            return X[:, bass.ds((t + ahead) % TILES if ahead else t, 1), :].rearrange("p o d -> p (o d)")

        def stats_step(dve, v0, t, s, ahead=0):
            slot = (s + ahead) % SLOTS
            v = v0 + t + ahead
            if v0 or v >= TILES:
                dve.wait_ge(x_updated, v - TILES + 1)
            elif v < BLK:
                dve.wait_ge(x_first_in[v // 2], 16)
            else:
                dve.wait_ge(x_in_sem[v // BLK], 16)
            if v0 or v >= SLOTS:
                dve.wait_ge(norm_done, v - SLOTS + 1)
            nc.vector.bn_stats(bnst[:, slot, :], x_tile(t, ahead)).then_inc(stats_raw, 1)

        def stats_halves_written(dve, v0, t, ahead=0):
            dve.wait_ge(stats_raw, v0 + t + ahead + 1)

        def aggregate_step(s, ahead=0):
            slot = (s + ahead) % SLOTS
            nc.vector.bn_aggr(mv[:, slot, :], bnst[:, slot, :]).then_inc(stats_ready, 1)

        def rstd_step(pool, v0, t, s, ahead=0):
            slot = (s + ahead) % SLOTS
            v = v0 + t + ahead
            pool.wait_ge(stats_ready, v + 1)
            nc.gpsimd.tensor_tensor(minus_mean[:, slot, :], mv[:, slot, 0:1], consts[:, 2:3], ALU.mult
                                    ).then_inc(mean_negated, 1)
            nc.gpsimd.tensor_tensor(veps[:, slot, :], mv[:, slot, 1:2], consts[:, 0:1], ALU.add).then_inc(eps_added, 1)
            pool.wait_ge(eps_added, v + 1)
            nc.gpsimd.tensor_tensor(rstd[:, slot, :], veps[:, slot, :], consts[:, 1:2], ALU.pow).then_inc(rstd_made, 1)
            pool.wait_ge(rstd_made, v + 1)
            pool.wait_ge(mean_negated, v + 1)
            nc.gpsimd.tensor_tensor(nmr[:, slot, :], minus_mean[:, slot, :], rstd[:, slot, :], ALU.mult
                                    ).then_inc(rstd_ready, 1)

        def norm_step(act, v0, t, s, ahead=0):
            slot = (s + ahead) % SLOTS
            v = v0 + t + ahead
            if v0 or v >= SLOTS:
                act.wait_ge(transposed, v - SLOTS + 1)
            act.wait_ge(rstd_ready, v + 1)
            nc.scalar.activation(LN[:, slot, :], x_tile(t, ahead), ACT.Identity, bias=nmr[:, slot, :],
                                 scale=rstd[:, slot, :]).then_inc(norm_done, 1)

        def transpose_step(pe, v0, t, s, ahead=0):
            slot = (s + ahead) % SLOTS
            pe.wait_ge(norm_done, v0 + t + ahead + 1)
            for j in range(KT):
                last = nc.tensor.transpose(front[slot][:, j * P:(j + 1) * P],
                                           LN[:, slot, j * P:(j + 1) * P], ident[:])
            last.then_inc(transposed, 1)

        def bank(slot):
            return front[slot][:, :].rearrange("p (j r) -> p j r", j=KT)

        def xt_hi_step(act, v0, t, s, ahead=0):
            slot = (s + ahead) % SLOTS
            act.wait_ge(transposed, v0 + t + ahead + 1)
            nc.scalar.activation(XTh[:, :, slot, :], bank(slot), ACT.Copy).then_inc(xt_hi_done, 1)

        def xt_lo_step(dve, v0, t, s, ahead=0):
            slot = (s + ahead) % SLOTS
            dve.wait_ge(xt_hi_done, v0 + t + ahead + 1)
            nc.vector.tensor_tensor(XTl[:, :, slot, :], bank(slot), XTh[:, :, slot, :].bitcast(F32),
                                    ALU.subtract).then_inc(xt_ready, 1)

        def update_step(dve, v0, t, a, scale):
            dve.wait_ge(acc_ready, v0 + t + 1)
            xt = x_tile(t)
            if scale == 1.0:
                nc.vector.tensor_tensor(xt, acc[a][:], xt, ALU.add).then_inc(x_updated, 1)
            else:
                nc.vector.scalar_tensor_tensor(out=xt, in0=acc[a][:], scalar=scale, in1=xt,
                                               op0=ALU.mult, op1=ALU.add).then_inc(x_updated, 1)

        @block.sync
        def _(sp):
            sp.dma_start(par[:], params).then_inc(params_in, 16)
            def load_first_x(h):
                two = slice(2 * h, 2 * h + 2)
                sp.dma_start(X[:, two, :], x_v[:, two, :]).then_inc(x_first_in[h], 16)

            def load_quantised(j):
                sp.dma_start(qraw[:, j, :], qweight[:, j, :]).then_inc(quant_in[j], 16)

            load_first_x(0)
            sp.dma_start(qsh[:], qshift).then_inc(rows_in, 16)
            sp.dma_start(zsB[:], qrows.partition_broadcast(P)).then_inc(rows_in, 16)
            load_quantised(0)
            sp.dma_start(ident[:], table_in[:, IDENT:IDENT + P]).then_inc(ident_in, 16)
            load_first_x(1)
            for j in range(1, KT):
                load_quantised(j)
            sp.dma_start(X[:, BLK:2 * BLK, :], x_v[:, BLK:2 * BLK, :]).then_inc(x_in_sem[1], 16)
            sp.dma_start(biasB[:], qbias.partition_broadcast(P)).then_inc(bias_in, 16)
            sp.dma_start(om[:], omega_in.partition_broadcast(P)).then_inc(omega_in_sem, 16)
            sp.dma_start(tab[:], table_in).then_inc(tables_in, 16)
            sp.dma_start(X[:, 2 * BLK:3 * BLK, :], x_v[:, 2 * BLK:3 * BLK, :]).then_inc(x_in_sem[2], 16)
            sp.dma_start(cosT[:], cos_in).then_inc(waves_in, 16)
            sp.dma_start(sinT[:], sin_in).then_inc(waves_in, 16)
            sp.dma_start(X[:, 3 * BLK:4 * BLK, :], x_v[:, 3 * BLK:4 * BLK, :]).then_inc(x_in_sem[3], 16)

            def load_chunk(c, parity):
                cols = bass.ds(c * CHUNK, CHUNK)
                sp.dma_start(G[:, parity, :], wffn[:, cols]).then_inc(chunk_in[parity], 16)

            load_chunk(0, 0)
            load_chunk(1, 1)
            with sp.Fori(1, POOL_CHUNKS // 2 + 1) as pair:
                for parity in range(2):
                    sp.wait_ge(split_by_pool, pair * 2 + parity - 1)
                    load_chunk(pair * 2 + parity, parity)
            with sp.Fori(1, (NCHUNK - POOL_CHUNKS) // 2) as pair:
                for parity in range(2):
                    sp.wait_ge(split_by_dve, pair * 2 + parity - 1)
                    load_chunk(POOL_CHUNKS + pair * 2 + parity, parity)
            for b in range(TILES // BLK - 1):
                sp.wait_ge(x_updated, 5 * TILES + (b + 1) * BLK)
                sp.dma_start(out_v[:, b * BLK:(b + 1) * BLK, :], X[:, b * BLK:(b + 1) * BLK, :]).then_inc(stored, 16)
            for t in range(TILES - BLK, TILES):
                sp.wait_ge(x_updated, 5 * TILES + t + 1)
                sp.dma_start(out_v[:, t:t + 1, :], X[:, t:t + 1, :]).then_inc(stored, 16)
            sp.wait_ge(stored, 16 * (TILES // BLK - 1 + BLK))

        @block.gpsimd
        def _(pool):
            TT = nc.gpsimd.tensor_tensor
            values = (EPS, -0.5, -1.0, float(np.e), 2.0)
            for i, value in enumerate(values):
                nc.gpsimd.memset(consts[:, i:i + 1], value).then_inc(const_ready, 1)
            nc.gpsimd.memset(rhs1[:], 0.0).then_inc(const_ready, 1)
            nc.gpsimd.memset(rhs2[:], 0.0).then_inc(const_ready, 1)
            assert len(values) == CONST_COLUMNS
            pool.wait_ge(const_ready, CONST_COLUMNS + 2)
            minus, euler, two = consts[:, 2:3], consts[:, 3:4], consts[:, 4:5]

            chain = [0]

            def link(ins):
                chain[0] += 1
                ins.then_inc(setup_pool, 1)
                pool.wait_ge(setup_pool, chain[0])

            def col(c):
                return par[:, c:c + 1]

            pool.wait_ge(params_in, 16)
            a2, nlr, nli, nal, inv, neg = (small[:, i:i + 1] for i in (1, 2, 3, 8, 9, 10))
            TT(nlr, col(LAM_R), minus, ALU.mult)
            TT(nli, col(LAM_I), minus, ALU.mult)
            link(TT(neg, col(LOGSTEP), minus, ALU.mult))
            link(TT(inv, euler, neg, ALU.pow))
            link(TT(a2, inv, two, ALU.mult))
            link(TT(inv, a2, col(LAM_R), ALU.add))
            TT(nal, inv, minus, ALU.mult).then_inc(coef_ready, 1)

            for t in range(SLOTS):
                rstd_step(pool, 0, t, t)

            for j in range(KT):
                pool.wait_ge(dequant_hi, j + 1)
                TT(Ql[:, j, :], wq[:, j, :], Qh[:, j, :].bitcast(F32), ALU.subtract).then_inc(dequant_split, 1)

            for t in range(SLOTS, RSTD_AHEAD):
                rstd_step(pool, 0, t, t % SLOTS)

            def bias_step(v0, t):
                pool.wait_ge(norm_done, v0 + t + 1)
                nc.gpsimd.tensor_tensor(x_tile(t), x_tile(t), biasB[:], ALU.add).then_inc(bias_added, 1)

            def chunk_lo_step(c, parity):
                pool.wait_ge(chunk_hi, c + 1)
                cols = bass.ds(c * CHUNK, CHUNK)
                nc.gpsimd.tensor_tensor(Wl[:, cols], G[:, parity, :], Wh[:, cols].bitcast(F32),
                                        ALU.subtract).then_inc(split_by_pool, 1)

            NUMERATORS_AT = 1

            def numerators():
                pool.wait_ge(b_ready, 1)
                for a, (ur, ui) in enumerate(((CT_R, CT_I), (Q_R, Q_I))):
                    wide = lambda c: col(c).to_broadcast([P, 2])
                    TT(part[:, 0, :], vec[:, 0, :], wide(ur), ALU.mult)
                    TT(part[:, 1, :], vec[:, 1, :], wide(ui), ALU.mult)
                    TT(part[:, 2, :], vec[:, 1, :], wide(ur), ALU.mult)
                    link(TT(part[:, 3, :], vec[:, 0, :], wide(ui), ALU.mult))
                    TT(num_r[:, a, :], part[:, 0, :], part[:, 1, :], ALU.add)
                    link(TT(num_i[:, a, :], part[:, 2, :], part[:, 3, :], ALU.subtract))
                pool.wait_ge(rstd_ready, NUMERATORS_AT + RSTD_AHEAD + 1)
                for layer in range(2):
                    rows = slice(layer * NS, layer * NS + NS)
                    nr = num_r[rows, :, :].rearrange("p a b -> p (a b)")
                    ni = num_i[rows, :, :].rearrange("p a b -> p (a b)")
                    nc.gpsimd.tensor_copy(rhs1[rows, layer, 0:4], nr).then_inc(numer_ready, 1)
                    nc.gpsimd.tensor_copy(rhs1[rows, layer, 4:8], ni).then_inc(numer_ready, 1)
                    nc.gpsimd.tensor_copy(rhs2[rows, layer, 0:4], ni).then_inc(numer_ready, 1)
                    TT(rhs2[rows, layer, 4:8], nr, minus[rows, :].to_broadcast([NS, 4]), ALU.mult
                       ).then_inc(numer_ready, 1)
                    pool.wait_ge(numer_ready, (layer + 1) * 4)

            def invert(c):
                cols = slice(c * P, (c + 1) * P)
                pool.wait_ge(den_recip, c + 1)
                TT(Rr[:, cols], den_r[:, cols], tmp[:, cols], ALU.mult).then_inc(inv_den_ready, 1)
                TT(Ri[:, cols], den_i[:, cols], tmp[:, cols], ALU.mult).then_inc(inv_den_ready, 1)

            pool.wait_ge(bias_ready, 1)
            for t in range(TILES):
                bias_step(0, t)
                rstd_step(pool, 0, t, t % SLOTS, RSTD_AHEAD)
                if t == NUMERATORS_AT:
                    numerators()
                if t == 2:
                    pool.wait_ge(den_squared, 2)
                    TT(mag[:], mag[:], tmp[:], ALU.add).then_inc(mag_ready, 1)
                if t in range(4, 4 + KT):
                    invert(t - 4)

            def light(stage, first, last, chunks, chunk0):
                kind, _ = LIGHT[stage]
                v0 = stage * TILES
                with pool.Fori(first // SLOTS, last // SLOTS) as grp:
                    t = grp * SLOTS
                    for s in range(SLOTS):
                        if kind == "quant":
                            bias_step(v0, t + s)
                        rstd_step(pool, v0, t + s, s, RSTD_AHEAD)
                        for i in range(chunks):
                            c = s * chunks + i
                            chunk_lo_step(chunk0 + t * chunks + c, c % 2)

            for run in WEIGHT_VISITS[1]:
                light(1, *run)
            light(2, *NO_WEIGHTS)

            def ffn(stage, first, last):
                v0 = stage * TILES
                with pool.Fori(first // SLOTS, last // SLOTS) as grp:
                    t = grp * SLOTS
                    for s in range(BLK):
                        rstd_step(pool, v0, t + s, s, RSTD_AHEAD)

            ffn(3, 0, TILES)
            light(4, *NO_WEIGHTS)
            ffn(5, 0, TILES - BLK)

        @block.scalar
        def _(act):
            def chunk_hi_step(c, parity):
                act.wait_ge(chunk_in[parity], 16 * (c // 2 + 1) if isinstance(c, int) else c * 8 + 16 - 8 * parity)
                cols = bass.ds(c * CHUNK, CHUNK)
                nc.scalar.activation(Wh[:, cols], G[:, parity, :], ACT.Copy).then_inc(chunk_hi, 1)

            def den_scale():
                act.wait_ge(coef_ready, 1)
                act.wait_ge(omega_in_sem, 16)
                nc.scalar.activation(den_r[:], om[:, 0, :], ACT.Copy, scale=small[:, 1:2]).then_inc(den_scaled, 1)
                nc.scalar.activation(den_i[:], om[:, 2, :], ACT.Copy, scale=small[:, 8:9]).then_inc(den_scaled, 1)

            def den_square():
                act.wait_ge(den_ready, 2)
                nc.scalar.activation(mag[:], den_r[:], ACT.Square).then_inc(den_squared, 1)
                nc.scalar.activation(tmp[:], den_i[:], ACT.Square).then_inc(den_squared, 1)

            def toe_round(layer):
                act.wait_ge(toe_ready, layer + 1)
                nc.scalar.activation(TOEh[:, layer, :], toe[:, layer, :], ACT.Copy).then_inc(toe_hi, 1)

            def dequant_round(j):
                act.wait_ge(dequant_ready, j + 1)
                nc.scalar.activation(Qh[:, j, :], wq[:, j, :], ACT.Copy).then_inc(dequant_hi, 1)

            act.wait_ge(const_ready, CONST_COLUMNS + 2)
            nc.scalar.activation(silu_warm[:], consts[:, 0:1], ACT.Silu)
            act.wait_ge(rows_in, 32)
            nc.scalar.activation(zsB[:, 1, :], zsB[:, 1, :], ACT.Copy, scale=0.5).then_inc(scale_halved, 1)
            norm_step(act, 0, 0, 0)
            norm_step(act, 0, 1, 1)
            for j in range(KT):
                dequant_round(j)
                xt_hi_step(act, 0, j, j)
                if j < 2:
                    norm_step(act, 0, j + 2, j + 2)
            norm_step(act, 0, SLOTS, 0)
            act.wait_ge(bias_in, 16)
            nc.scalar.activation(biasB[:], biasB[:], ACT.Copy, scale=0.5).then_inc(bias_ready, 1)
            den_scale()

            def visit(v0, t, s):
                act.wait_ge(acc_ready, v0 + t + 1)
                xt_hi_step(act, v0, t, s, XT_AHEAD)
                norm_step(act, v0, t, s, NORM_AHEAD)

            for t in range(TILES):
                visit(0, t, t % SLOTS)
                if t == 1:
                    den_square()
                if t in (13, 14):
                    toe_round(t - 13)

            def light(stage, first, last, chunks, chunk0):
                v0 = stage * TILES
                with act.Fori(first // SLOTS, last // SLOTS) as grp:
                    t = grp * SLOTS
                    for s in range(SLOTS):
                        visit(v0, t + s, s)
                        if chunks and stage == 1:
                            act.wait_ge(toe_split, 2)
                        for i in range(chunks):
                            c = s * chunks + i
                            chunk_hi_step(chunk0 + t * chunks + c, c % 2)

            for stage in WEIGHT_VISITS:
                for run in WEIGHT_VISITS[stage]:
                    light(stage, *run)
            act.wait_ge(acc_ready, 3 * TILES)
            act.wait_ge(bias_added, 2 * TILES)
            for c in range(EARLY_CHUNKS, NCHUNK):
                chunk_hi_step(c, c % 2)

            def ffn(stage, first, last, ahead=True):
                v0 = stage * TILES
                k0 = BLOCKS_BEFORE[stage]
                with act.Fori(first // SLOTS, last // SLOTS) as grp:
                    t = grp * SLOTS
                    for f in range(FT):
                        m = fwidth(f)
                        n = (k0 * FT + f) + grp * FT
                        act.wait_ge(gate_ready, n + 1)
                        if stage == 3:
                            if f < 2:
                                act.wait_ge(split_by_dve, NCHUNK - POOL_CHUNKS)
                        if stage != 3 or f >= 2:
                            act.wait_ge(hid_ready, n - 1)
                        nc.scalar.activation(G[:m, f % 2, 0:D], front[2 * (f % 2)][:m, :], ACT.Silu
                                             ).then_inc(silu_done, 1)
                        act.wait_ge(prod_done, n + 1)
                        if f == 1:
                            act.wait_ge(acc_ready, v0 + t)
                        elif f >= 2:
                            act.wait_ge(down_done, (FT - 1) * (k0 + grp) + f - 1)
                        elif stage == 5:
                            act.wait_ge(down_done, (FT - 1) * (k0 + grp))
                        nc.scalar.activation(Hh[:m, f % 2, :], G[:m, f % 2, 0:D], ACT.Copy).then_inc(hid_hi_done, 1)
                        if 3 <= f < 6 and ahead:
                            norm_step(act, v0, t + f - 3, f - 3, NORM_AHEAD)
                    for s in range(BLK):
                        if ahead:
                            xt_hi_step(act, v0, t + s, s, XT_AHEAD)
                    if ahead:
                        norm_step(act, v0, t + 3, 3, NORM_AHEAD)

            ffn(3, 0, TILES)
            light(4, *NO_WEIGHTS)
            ffn(5, 0, TILES - BLK)
            ffn(5, TILES - BLK, TILES, ahead=False)

        @block.vector
        def _(dve):
            chain = [0]

            def link(ins):
                chain[0] += 1
                ins.then_inc(setup_dve, 1)
                dve.wait_ge(setup_dve, chain[0])

            V = nc.vector

            def col(c):
                return par[:, c:c + 1]

            nlr, nli = small[:, 2:3], small[:, 3:4]
            dve.wait_ge(params_in, 16)
            vc = par[:, VC0:VC0 + 2 * NS].rearrange("p (c m) -> p c m", c=2)
            bp = par[:, BP0:BP0 + NS].unsqueeze(1).to_broadcast([P, 2, NS])
            V.tensor_copy(vec[:, 0, 1:2], col(P_R))
            V.tensor_copy(vec[:, 1, 1:2], col(P_I))
            link(V.tensor_tensor(bprod[:], vc, bp, ALU.mult))
            V.tensor_reduce(vec[:, :, 0:1], bprod[:], AX.X, ALU.add).then_inc(b_ready, 1)

            def dequantise(j):
                dve.wait_ge(quant_in[j], 16)
                link(V.tensor_scalar(qraw[:, j, :], qraw[:, j, :], qsh[:, 0:1], 63,
                                     ALU.logical_shift_right, ALU.bitwise_and))
                link(V.tensor_tensor(wq[:, j, :], qraw[:, j, :], zsB[:, 0, :], ALU.subtract))
                V.tensor_tensor(wq[:, j, :], wq[:, j, :], zsB[:, 1, :], ALU.mult).then_inc(dequant_ready, 1)

            def early_stats(t):
                stats_step(dve, 0, t, t % SLOTS)
                stats_halves_written(dve, 0, t)
                aggregate_step(t % SLOTS)

            early_stats(0)
            early_stats(1)
            dve.wait_ge(rows_in, 32)
            dve.wait_ge(scale_halved, 1)
            dequantise(0)
            early_stats(2)
            early_stats(3)
            dequantise(1)
            dequantise(2)
            xt_lo_step(dve, 0, 0, 0)
            dequantise(3)
            xt_lo_step(dve, 0, 1, 1)
            early_stats(4)
            xt_lo_step(dve, 0, 2, 2)
            xt_lo_step(dve, 0, 3, 3)
            for t in range(SLOTS + 1, STATS_AHEAD):
                early_stats(t)

            def denominators_re():
                dve.wait_ge(den_scaled, 2)
                link(V.scalar_tensor_tensor(out=den_r[:], in0=om[:, 1, :], scalar=nlr, in1=den_r[:],
                                            op0=ALU.mult, op1=ALU.add))
                V.scalar_tensor_tensor(out=den_r[:], in0=om[:, 2, :], scalar=col(LAM_I), in1=den_r[:],
                                       op0=ALU.mult, op1=ALU.add).then_inc(den_ready, 1)

            def denominators_im():
                V.scalar_tensor_tensor(out=den_i[:], in0=om[:, 1, :], scalar=nli, in1=den_i[:],
                                       op0=ALU.mult, op1=ALU.add).then_inc(den_ready, 1)

            def reciprocal(c):
                cols = slice(c * P, (c + 1) * P)
                dve.wait_ge(mag_ready, 1)
                V.reciprocal(tmp[:, cols], mag[:, cols]).then_inc(den_recip, 1)

            def k(a, b, ri):
                return kk[:, :, :, 4 * ri + 2 * a + b]

            n = [tab[:, NPLUS + ri * KT:NPLUS + (ri + 1) * KT].unsqueeze(2).to_broadcast([P, KT, 2]) for ri in range(2)]
            w = [cm[:, i] for i in range(16)]

            def cmul(o_r, o_i, ar, ai, br, bi):
                V.tensor_tensor(w[12], ar, br, ALU.mult)
                V.tensor_tensor(w[13], ai, bi, ALU.mult)
                V.tensor_tensor(w[14], ar, bi, ALU.mult)
                link(V.tensor_tensor(w[15], ai, br, ALU.mult))
                V.tensor_tensor(o_r, w[12], w[13], ALU.subtract)
                link(V.tensor_tensor(o_i, w[14], w[15], ALU.add))


            def resolvent():
                dve.wait_ge(cauchy_ready, 1)
                dve.wait_ge(tables_in, 16)
                link(V.tensor_copy(kk[:].rearrange("p c l e -> p (c l e)"), acc[2][:, 0:KT * 16]))
                cmul(w[0], w[1], k(1, 1, 0), k(1, 1, 1), n[0], n[1])
                link(V.tensor_scalar(w[0], w[0], 1.0, None, ALU.add))
                V.tensor_tensor(w[2], w[0], w[0], ALU.mult)
                link(V.tensor_tensor(w[3], w[1], w[1], ALU.mult))
                link(V.tensor_tensor(w[2], w[2], w[3], ALU.add))
                link(V.reciprocal(w[3], w[2]))
                V.tensor_tensor(w[0], w[0], w[3], ALU.mult)
                link(V.scalar_tensor_tensor(out=w[1], in0=w[1], scalar=-1.0, in1=w[3], op0=ALU.mult, op1=ALU.mult))

            def roots():
                cmul(w[4], w[5], k(0, 1, 0), k(0, 1, 1), k(1, 0, 0), k(1, 0, 1))
                cmul(w[6], w[7], w[4], w[5], n[0], n[1])
                cmul(w[8], w[9], w[6], w[7], w[0], w[1])
                V.tensor_tensor(w[10], k(0, 0, 0), w[8], ALU.subtract)
                link(V.tensor_tensor(w[11], k(0, 0, 1), w[9], ALU.subtract))
                V.tensor_scalar(at_r[:], w[10], 2.0 / D, None, ALU.mult)
                link(V.tensor_scalar(at_i[:], w[11], 2.0 / D, None, ALU.mult))

            even, odd = fold[:, 4], fold[:, 5]

            def fold_roots():
                apart = tab[:, FOLD:FOLD + HALF].unsqueeze(2).to_broadcast([P, HALF, 2])
                r, r_, i, i_ = at_r[:, 0:HALF], at_r[:, HALF:KT], at_i[:, 0:HALF], at_i[:, HALF:KT]
                V.tensor_tensor(fold[:, 0], r_, apart, ALU.mult)
                link(V.tensor_tensor(fold[:, 1], i, i_, ALU.subtract))
                V.tensor_tensor(even, r, fold[:, 0], ALU.add)
                V.tensor_tensor(fold[:, 2], fold[:, 1], apart, ALU.mult)
                link(V.tensor_tensor(fold[:, 3], r_, fold[:, 0], ALU.subtract))
                link(V.tensor_tensor(odd, fold[:, 2], fold[:, 3], ALU.add))

            def twist(layer):
                for c in range(HALF):
                    e, o = even[:, c, layer:layer + 1], odd[:, c, layer:layer + 1]
                    c1, sn, c2 = (tab[:, at + c * P:at + (c + 1) * P] for at in (TWIST_C1, TWIST_S, TWIST_C2))
                    V.tensor_scalar(tw[:, 0, :], sn, o, None, ALU.mult)
                    link(V.tensor_scalar(tw[:, 1, :], c2, o, None, ALU.mult))
                    V.scalar_tensor_tensor(out=A1[:, layer, c, :], in0=c1, scalar=e, in1=tw[:, 0, :],
                                           op0=ALU.mult, op1=ALU.add)
                    last = V.scalar_tensor_tensor(out=A2[:, layer, c, :], in0=sn, scalar=e, in1=tw[:, 1, :],
                                                  op0=ALU.mult, op1=ALU.subtract)
                    if c < HALF - 1:
                        link(last)
                last.then_inc(twisted_ready, 1)

            def strip(layer):
                dve.wait_ge(toeplitz_sum, layer + 1)
                link(V.tensor_copy(toe[:, layer, :], acc[2 + layer][:]))
                link(V.tensor_tensor(toe[:, layer, 0:P], toe[:, layer, 0:P], tab[:, CAUSAL:CAUSAL + P], ALU.mult))
                V.scalar_tensor_tensor(out=toe[:, layer, 0:P], in0=tab[:, IDENT:IDENT + P], scalar=col(D_0 + layer),
                                       in1=toe[:, layer, 0:P], op0=ALU.mult, op1=ALU.add).then_inc(toe_ready, 1)

            def strip_lo(layer):
                dve.wait_ge(toe_hi, layer + 1)
                V.tensor_tensor(TOEl[:, layer, :], toe[:, layer, :], TOEh[:, layer, :].bitcast(F32),
                                ALU.subtract).then_inc(toe_split, 1)

            def visit(v0, t, s, biased, a):
                stats_step(dve, v0, t, s, STATS_AHEAD)
                if biased is not None:
                    dve.wait_ge(bias_added, biased)
                stats_halves_written(dve, v0, t, STATS_AHEAD)
                update_step(dve, v0, t, a, 1.0)
                xt_lo_step(dve, v0, t, s, XT_AHEAD)
                aggregate_step(s, STATS_AHEAD)

            for t in range(TILES):
                visit(0, t, t % SLOTS, t + 1, t % 2)
                if t == 0:
                    denominators_re()
                if t == 1:
                    denominators_im()
                if t in range(3, 3 + KT):
                    reciprocal(t - 3)
                if t == 8:
                    resolvent()
                if t == 9:
                    roots()
                if t == 10:
                    fold_roots()
                    twist(0)
                if t == 11:
                    twist(1)
                if t in (14, 15):
                    strip_lo(t - 14)
                if t in (13, 14):
                    strip(t - 13)

            def chunk_lo_step(c, parity):
                dve.wait_ge(chunk_hi, c + 1)
                cols = bass.ds(c * CHUNK, CHUNK)
                V.tensor_tensor(Wl[:, cols], G[:, parity, :], Wh[:, cols].bitcast(F32),
                                ALU.subtract).then_inc(split_by_dve, 1)

            def light(stage, first, last, chunks, chunk0):
                kind, _ = LIGHT[stage]
                v0 = stage * TILES
                with dve.Fori(first // SLOTS, last // SLOTS) as grp:
                    t = grp * SLOTS
                    for s in range(SLOTS):
                        biased = BIAS_BEFORE[stage] + t + s + 1 if kind == "quant" else None
                        visit(v0, t + s, s, biased, sum_bank(stage, s))
                        for i in range(chunks):
                            c = s * chunks + i
                            chunk_lo_step(chunk0 + t * chunks + c, c % 2)

            def ffn(stage, first, last, ahead=True):
                v0 = stage * TILES
                k0 = BLOCKS_BEFORE[stage]
                with dve.Fori(first // SLOTS, last // SLOTS) as grp:
                    t = grp * SLOTS
                    for f in range(FT):
                        m = fwidth(f)
                        n_ = (k0 * FT + f) + grp * FT
                        dve.wait_ge(up_ready, n_ + 1)
                        dve.wait_ge(silu_done, n_ + 1)
                        g = G[:m, f % 2, 0:D]
                        V.tensor_tensor(g, front[2 * (f % 2) + 1][:m, :], g, ALU.mult).then_inc(prod_done, 1)
                        if 2 <= f < 6 and ahead:
                            stats_step(dve, v0, t + f - 2, f - 2, STATS_AHEAD)
                            stats_halves_written(dve, v0, t + f - 2, STATS_AHEAD)
                        dve.wait_ge(hid_hi_done, n_ + 1)
                        V.tensor_tensor(Hl[:m, f % 2, :], g, Hh[:m, f % 2, :].bitcast(F32),
                                        ALU.subtract).then_inc(hid_ready, 1)
                        if 2 <= f < 6 and ahead:
                            aggregate_step(f - 2, STATS_AHEAD)
                    for s in range(BLK):
                        if ahead:
                            xt_lo_step(dve, v0, t + s, s, XT_AHEAD)
                    for s in range(BLK):
                        update_step(dve, v0, t + s, s, 0.5)

            light(1, *NO_WEIGHTS)
            for run in WEIGHT_VISITS[2]:
                light(2, *run)
            for c in range(EARLY_CHUNKS, NCHUNK):
                chunk_lo_step(c, c % 2)
            ffn(3, 0, TILES)
            light(4, *NO_WEIGHTS)
            ffn(5, 0, TILES - BLK)
            ffn(5, TILES - BLK, TILES, ahead=False)

        @block.tensor
        def _(pe):
            T = nc.tensor
            pe.wait_ge(ident_in, 16)
            for t in range(XT_AHEAD):
                transpose_step(pe, 0, t, t)

            def products(stage, s, a):
                kind, layer = LIGHT[stage]
                for j in range(KT):
                    if kind == "quant":
                        wh, wl, lo = Qh[:, j, :], Ql[:, j, :], 0
                        if stage == 0:
                            pe.wait_ge(dequant_split, j + 1)
                    else:
                        wh, wl, lo = TOEh[:, layer, 0:D - j * P], TOEl[:, layer, 0:D - j * P], j * P
                    o = acc[a][:, lo:D]
                    xh, xl = XTh[:, j, s, :], XTl[:, j, s, :]
                    T.matmul(o, xh, wh, start=(j == 0), stop=False)
                    T.matmul(o, xh, wl, start=False, stop=False)
                    last = T.matmul(o, xl, wh, start=False, stop=(j == KT - 1))
                last.then_inc(acc_ready, 1)

            def cauchy():
                pe.wait_ge(inv_den_ready, 2 * KT)
                pe.wait_ge(numer_ready, 8)
                for c in range(KT):
                    o = acc[2][:, c * 16:(c + 1) * 16]
                    T.matmul(o, Rr[:, c * P:(c + 1) * P], rhs1[:].rearrange("p l e -> p (l e)"), start=True, stop=False)
                    last = T.matmul(o, Ri[:, c * P:(c + 1) * P], rhs2[:].rearrange("p l e -> p (l e)"),
                                    start=False, stop=True)
                last.then_inc(cauchy_ready, 1)

            def toeplitz(layer):
                pe.wait_ge(twisted_ready, layer + 1)
                pe.wait_ge(waves_in, 32)
                for c in range(HALF):
                    T.matmul(acc[2 + layer][:], A1[:, layer, c, :], cosT[:, c, :], start=(c == 0), stop=False)
                    last = T.matmul(acc[2 + layer][:], A2[:, layer, c, :], sinT[:, c, :], start=False,
                                    stop=(c == HALF - 1))
                last.then_inc(toeplitz_sum, 1)

            for t in range(TILES):
                pe.wait_ge(xt_ready, t + 1)
                if t >= 2:
                    pe.wait_ge(x_updated, t - 1)
                products(0, t % SLOTS, t % 2)
                transpose_step(pe, 0, t, t % SLOTS, XT_AHEAD)
                if t == 8:
                    cauchy()
                if t == 12:
                    toeplitz(0)
                    toeplitz(1)

            def light(stage):
                kind, layer = LIGHT[stage]
                v0 = stage * TILES
                with pe.Fori(0, TILES // SLOTS) as grp:
                    t = grp * SLOTS
                    for s in range(SLOTS):
                        v = v0 + t + s
                        pe.wait_ge(xt_ready, v + 1)
                        if kind == "conv":
                            pe.wait_ge(toe_split, layer + 1)
                        pe.wait_ge(x_updated, v - SLOTS + 1)
                        if stage == 1 and s == 1:
                            pe.wait_ge(toe_ready, 2)
                        products(stage, s, sum_bank(stage, s))
                        transpose_step(pe, v0, t + s, s, XT_AHEAD)

            def ffn(stage, first, last_t, ahead=True):
                opening = first == 0
                v0 = stage * TILES
                k0 = BLOCKS_BEFORE[stage]
                with pe.Fori(first // SLOTS, last_t // SLOTS) as grp:
                    t = grp * SLOTS

                    def hidden_sums(f, which, w0, tiles):
                        m = fwidth(f)
                        o = front[2 * (f % 2) + which][:m, tiles.start * P:tiles.stop * P]
                        for j in range(KT):
                            cols = slice(w0 + j * F + f * P, w0 + j * F + f * P + m)
                            xh = XTh[:, j, tiles, :].rearrange("p s r -> p (s r)")
                            xl = XTl[:, j, tiles, :].rearrange("p s r -> p (s r)")
                            T.matmul(o, Wh[:, cols], xh, start=(j == 0), stop=False)
                            T.matmul(o, Wh[:, cols], xl, start=False, stop=False)
                            last = T.matmul(o, Wl[:, cols], xh, start=False, stop=(j == KT - 1))
                        return last

                    def gate_up(f):
                        if f == 0 and opening:
                            hidden_sums(f, 0, GATE0, slice(0, BLK - 1))
                            pe.wait_ge(xt_ready, v0 + t + BLK)
                            hidden_sums(f, 0, GATE0, slice(BLK - 1, BLK)).then_inc(gate_ready, 1)
                        else:
                            hidden_sums(f, 0, GATE0, slice(0, BLK)).then_inc(gate_ready, 1)
                        hidden_sums(f, 1, UP0, slice(0, BLK)).then_inc(up_ready, 1)

                    def down(f):
                        m = fwidth(f)
                        cols = slice(DOWN0 + f * D, DOWN0 + (f + 1) * D)
                        pe.wait_ge(hid_ready, (k0 * FT + f + 1) + grp * FT)
                        if stage == 3:
                            pe.wait_ge(split_by_dve, chunks_up_to(DOWN0 + (f + 1) * D) - POOL_CHUNKS)
                        if f == 0:
                            pe.wait_ge(x_updated, v0 + t)
                        for r in range(BLK):
                            hh, hl = Hh[:m, f % 2, r * P:(r + 1) * P], Hl[:m, f % 2, r * P:(r + 1) * P]
                            T.matmul(acc[r][:], hh, Wh[:m, cols], start=(f == 0), stop=False)
                            T.matmul(acc[r][:], hh, Wl[:m, cols], start=False, stop=False)
                            last = T.matmul(acc[r][:], hl, Wh[:m, cols], start=False, stop=(f == FT - 1))
                            if f == FT - 1:
                                last.then_inc(acc_ready, 1)
                        if f < FT - 1:
                            last.then_inc(down_done, 1)

                    for f in range(FT):
                        if f == 0:
                            pe.wait_ge(xt_ready, v0 + t + (BLK - 1 if opening else BLK))
                            if stage == 3:
                                pe.wait_ge(split_by_pool, POOL_CHUNKS)
                                pe.wait_ge(split_by_dve, chunks_up_to(DOWN0) - POOL_CHUNKS)
                        if f >= 2:
                            pe.wait_ge(prod_done, (k0 * FT + f - 1) + grp * FT)
                        gate_up(f)
                        if f > 0:
                            down(f - 1)
                    if ahead:
                        pe.wait_ge(prod_done, (k0 * FT + FT) + grp * FT)
                        for s in range(BLK):
                            transpose_step(pe, v0, t + s, s, XT_AHEAD)
                    down(FT - 1)

            light(1)
            light(2)
            ffn(3, 0, BLK)
            ffn(3, BLK, TILES)
            light(4)
            ffn(5, 0, BLK)
            ffn(5, BLK, TILES - BLK)
            ffn(5, TILES - BLK, TILES, ahead=False)


def constants():
    half = D // 2
    w = np.arange(half)
    d = np.arange(D)
    rows = lambda a: a.reshape(-1, P, a.shape[-1]).transpose(1, 0, 2)
    f = lambda a: np.ascontiguousarray(a, dtype=np.float32)
    ang = 2 * np.pi * ((w[:, None] * d[None, :]) % D) / D
    cos, sin = np.cos(ang), np.sin(ang)
    freq = np.concatenate([w, np.concatenate([[half], D - w[1:]])])
    th = 2 * np.pi * freq / D
    wr, wi = np.cos(th), -np.sin(th)
    wi[freq == half] = 0.0
    c1, sn, c2 = cos[:, :P].copy(), sin[:, :P].copy(), cos[:, :P].copy()
    alternate = 1.0 - 2.0 * (d % 2)
    sin[0] = alternate
    c2[0] = -alternate[:P]
    apart = np.ones((half, 1))
    apart[0] = 0.0
    j, e = np.arange(P)[:, None], np.arange(P)[None, :]
    flat = lambda a: rows(a).reshape(P, -1)
    table = np.concatenate([e == j, e >= j, flat(c1), flat(sn), flat(c2),
                            flat((1 + wr)[:, None]), flat(wi[:, None]), flat(apart)], axis=1)
    return {
        "cos_in": f(rows(cos)), "sin_in": f(rows(sin)), "omega_in": f(np.stack([1 - wr, 1 + wr, wi])),
        "table_in": f(table), "qshift": np.tile(np.array([0, 6, 0, 0], np.int32), P // 4).reshape(P, 1),
    }


def layout(inp):
    a = {n: np.asarray(v) for n, v in inp.items()}
    rows = []
    for layer in ("L0", "L1"):
        g = lambda n: a[f"{layer}_attn_{n}"]
        col = lambda v: np.broadcast_to(v.reshape(-1, 1), (NS, 1))
        rows.append(np.concatenate([
            g("Lambda_ri"), g("p_ri"), g("q_ri"), g("Ct_ri").reshape(NS, 2), col(g("log_step")),
            col(a["L0_attn_D"]), col(a["L1_attn_D"]), col(np.zeros(1, np.float32)),
            g("Vc_ri").transpose(0, 2, 1).reshape(NS, 2 * NS),
            np.broadcast_to(g("Bp").reshape(1, NS), (NS, NS))], axis=1))
    k = np.arange(D)
    q = a["L0_ffn_qweight"].T[3 * (k // 4) + np.array([0, 0, 1, 2])[k % 4]]
    tiles = lambda w: w.reshape(KT, P, -1).transpose(1, 0, 2).reshape(P, -1)
    down = np.zeros((FT * P, D), np.float32)
    down[:F] = a["L1_ffn_W_down"].T
    down = down.reshape(FT, P, D).transpose(1, 0, 2).reshape(P, FT * D)
    wffn = np.concatenate([tiles(a["L1_ffn_W_gate"].T), tiles(a["L1_ffn_W_up"].T), down], axis=1)
    c = np.ascontiguousarray
    return {
        "x_in": c(a["L0_attn_u"]), "params": c(np.concatenate(rows, axis=0)),
        "qweight": c(q.reshape(KT, P, D).transpose(1, 0, 2)),
        "qrows": c(np.stack([a["L0_ffn_weight_zero_point"].reshape(D), a["L0_ffn_weight_scale"].reshape(D)])),
        "qbias": c(a["L0_ffn_bias"]), "wffn": c(wffn),
    } | constants()


_INS = ["x_in", "params", "qweight", "qshift", "qrows", "qbias", "wffn", "cos_in", "sin_in", "omega_in", "table_in"]


def kernel(**inputs):
    import concourse.bacc as _bacc
    from concourse.bass_utils import run_bass_kernel_spmd as _run

    nc = _bacc.Bacc("TRN2", target_bir_lowering=False, num_devices=1)
    arrays = layout(inputs)
    args = [nc.dram_tensor(n, arrays[n].shape, mybir.dt.from_np(arrays[n].dtype), kind="ExternalInput").ap()
            for n in _INS]
    args.append(nc.dram_tensor("out", (1, ROWS, D), F32, kind="ExternalOutput").ap())
    build(nc, *args)
    r = _run(nc, [arrays], core_ids=[0])
    return r.results[0]["out"]
```
